# Optimizing a Trainium2 kernel written in Bass

```python
import numpy as np
import jax
import jax.numpy as jnp

def _softmax(x, axis=-1):
    return jax.nn.softmax(x, axis=axis)

def _gelu(x):
    return jax.nn.gelu(x, approximate=True)

def _silu(x):
    return jax.nn.silu(x)

def _sigmoid(x):
    return jax.nn.sigmoid(x)

def _layernorm(x, axis=-1, eps=1e-05):
    m = jnp.mean(x, axis=axis, keepdims=True)
    v = jnp.var(x, axis=axis, keepdims=True)
    return (x - m) / jnp.sqrt(v + eps)

def _scatter_add(tgt, idx, src, axis=0):
    return tgt.at[idx].add(src)

def _segment_sum(src, seg, n):
    return jax.ops.segment_sum(src, seg, n)
kernel_name = 'mk_adj_preln_d1_adj_r2_48ab88'

def setup_inputs(seed: int=0):
    np.random.seed(seed)
    _w = jnp.asarray

    def _rec_inputs():
        import jax
        import jax.numpy as jnp
        _gk = jax.random.key(seed)
        x = -0.0005207 + 1.001 * jax.random.normal(jax.random.fold_in(_gk, 1), (8192, 128), jnp.float32)
        _w = (1.0 + jnp.arange(8192, dtype=jnp.float32)) ** (-0.5)
        _w = _w / _w.mean()
        _pij = jnp.clip(0.00195312 * _w[:, None] * _w[None, :], 0.0, 1.0)
        _a = jax.random.uniform(jax.random.fold_in(_gk, 2), (8192, 8192)) < _pij
        adj = _a.astype(jnp.int32)
        return (x, adj)
    x, adj = _rec_inputs()

    def _L0_gnn_setup():
        import jax, jax.numpy as jnp
        import numpy as np
        ALPHA = 0.2
        NEG_INF = -9000000000000000.0
        key = jax.random.key(seed)
        k1, k2, k3, k4 = jax.random.split(key, 4)
        N, F_in, F_out = (4096, 128, 128)
        x = jax.random.normal(k1, (N, F_in), dtype=jnp.float32)
        adj = jax.random.randint(k2, (N, N), 0, 2, dtype=jnp.int32)
        W = jax.random.normal(k3, (F_in, F_out), dtype=jnp.float32) * (1.0 / np.sqrt(F_in))
        a = jax.random.normal(k4, (2 * F_out, 1), dtype=jnp.float32) * 0.05
        return {'x': x, 'adj': adj, 'W': W, 'a': a}
    _L0_gnn_all = _L0_gnn_setup()
    _L0_gnn_in = {k: v for k, v in _L0_gnn_all.items() if k in ('W', 'a')}
    del _L0_gnn_all
    return {'x': x, 'adj': adj, 'L0_gnn_W': _L0_gnn_in['W'], 'L0_gnn_a': _L0_gnn_in['a']}

def reference(x, adj, L0_gnn_W, L0_gnn_a):
    import jax
    import jax.numpy as jnp

    def _L0_gnn_ref(x, adj, W, a):
        import jax, jax.numpy as jnp
        import numpy as np
        ALPHA = 0.2
        NEG_INF = -9000000000000000.0
        h = x @ W
        F_out = h.shape[1]
        a1 = a[:F_out, 0]
        a2 = a[F_out:, 0]
        s1 = h @ a1
        s2 = h @ a2
        e = jax.nn.leaky_relu(s1[:, None] + s2[None, :], negative_slope=ALPHA)
        scores = jnp.where(adj > 0, e, NEG_INF)
        attention = jax.nn.softmax(scores, axis=1)
        h_prime = attention @ h
        return jax.nn.elu(h_prime)
    h = jnp.maximum(_layernorm(x, axis=-1), 0.0)
    x = x + _L0_gnn_ref(h, adj, L0_gnn_W, L0_gnn_a)
    return x

_drawn_inputs = setup_inputs


def setup_inputs(seed=0):
    import zlib

    import numpy as np

    out = dict(_drawn_inputs(seed))
    spreads = {}
    factors = {}
    for name, (base, spread) in spreads.items():
        noise = np.random.default_rng([zlib.crc32(name.encode()), seed]).standard_normal(out[name].shape)
        drawn = base * np.exp(spread * noise) if base else spread * noise
        out[name] = jnp.asarray(drawn.astype(out[name].dtype))
    for name, factor in factors.items():
        out[name] = (out[name] * factor).astype(out[name].dtype)
    return out
```

```python
import concourse.bass as bass
from concourse import mybir
from contextlib import ExitStack

dt = mybir.dt
ALU = mybir.AluOpType
ACT = mybir.ActivationFunctionType
AX = mybir.AxisListType
RMAX = bass.bass_isa.ReduceOp.max

ALPHA = 0.2
EPS = 1e-5

PLUS, MINUS = 0x20, 0x10
NOEDGE = PLUS | MINUS
PLUS4, MINUS4 = PLUS * 0x01010101, MINUS * 0x01010101
MINUS_RESCALE = 4.0
FP16_TOP = 32768.0


def build(nc, x, adj, W, a, out):
    N, F = x.shape
    P = 128
    NB = N // P
    NQ = 4
    QC = N // NQ
    NH = 2
    CC = QC // NH
    NS = 4
    NT = CC // 128
    NK = 4
    NJ = NH * NT * NK
    NI = NB // 2
    CH = 2 * NH
    R = F + 1
    CW = CC // 4
    G = NJ // NK
    f32, f16, u32 = dt.float32, dt.float16, dt.uint32

    x_tiles = x.rearrange("(b p) f -> p b f", p=P)
    out_tiles = out.rearrange("(b p) f -> p b f", p=P)
    adj_view = adj.rearrange("(b s a) (g h c) -> g h a b s c", s=NS, a=32, g=NQ, h=NH)

    ctx = ExitStack()
    with ctx:
        def sb(name, shape, d):
            return ctx.enter_context(nc.sbuf_tensor(name, shape, d))

        def bank(name):
            return ctx.enter_context(nc.psum_tensor(name, [P, 512], f32))

        def sem(name):
            return ctx.enter_context(nc.semaphore(name))

        raw = sb("raw", [P, CH * NS * CC], dt.int32)
        noedge = sb("noedge", [P, NH, NS * CC], dt.uint8)
        code = sb("code", [P, NH, NS * CC], dt.int8)
        minus = sb("minus", [P, NH, NS * CW], u32)
        plus = sb("plus", [P, NH, NS * CW], u32)
        uv = sb("uv", [P, NJ, 4 * R], f16)
        s2row = sb("s2row", [P, QC], f32)
        s1bias = sb("s1bias", [P, NB, NS], f32)
        a_plus = sb("a_plus", [P, NB], f32)
        a_now = sb("a_now", [P, 2], f32)
        a_minus = sb("a_minus", [P, NB], f32)
        h_bound = sb("h_bound", [P, 1], f32)
        mean_h = sb("mean_h", [P, F], f32)
        scaled_plus = sb("scaled_plus", [P, 2, 2 * R], f32)
        both = sb("both", [P, 2, 2 * R], f32)
        sums = sb("sums", [P, 2, R], f32)
        empty = sb("empty", [P, 2], f32)
        den = sb("den", [P, 2], f32)
        rden = sb("rden", [P, 2], f32)
        rscale = sb("rscale", [P, 2], f32)
        ident = sb("ident", [P, P], f32)
        sel = sb("sel", [P, NS, NQ, 32], f32)
        ones = sb("ones", [P, P], f32)
        w_sb = sb("w_sb", [P, F], f32)
        w_t = sb("w_t", [P, F], f32)
        w_sq = sb("w_sq", [P, F], f32)
        a_sb = sb("a_sb", [P, 2], f32)
        wa = sb("wa", [P, 2], f32)
        wa2_rep = sb("wa2_rep", [P, 32], f32)
        stats = sb("stats", [P, NB, 6], f32)
        ln = sb("ln", [P, 8, NB], f32)
        colsum = sb("colsum", [P, 16], f32)
        colmean = sb("colmean", [P, 1], f32)
        colmean_rep = sb("colmean_rep", [P, P], f32)
        s1col = sb("s1col", [P, NB], f32)
        small = sb("small", [P, 8], f32)
        bexp = sb("bexp", [P, 2, NJ], f32)
        bscaled = sb("bscaled", [P, 2, NJ], f32)
        zmax = sb("zmax", [P, 3, NB], f32)
        hn = sb("hn", [P, 2, 4, F], f32)
        hn_set = sb("hn_set", [P, 4, 4 * P], f32)
        uv32 = sb("uv32", [P, 2, 2, 4, F], f32)

        slot_words = NS * CC
        raw_slot = [raw[:, q * slot_words:(q + 1) * slot_words].rearrange("p (s c) -> p s c", s=NS)
                    for q in range(CH)]
        x_sb = uv[:, :, :].rearrange("p j c -> p (j c)")[:, 0:2 * NB * F].bitcast(f32)\
            .rearrange("p (b f) -> p b f", f=F)
        hn_t = raw[:, 2 * slot_words:2 * slot_words + N].bitcast(f32)
        s2_turned = plus[:, :, :].rearrange("p h c -> p (h c)").bitcast(f32)\
            .rearrange("p (j a) -> p j a", a=32)
        fallback, y, ymin, yexp, elu1, xres, result = [
            uv32[:, i // 4, i // 2 % 2, 2 * (i % 2):2 * (i % 2) + 2, :] for i in range(7)]
        noedge_words = [noedge[:, h, :].bitcast(u32) for h in range(NH)]
        code_words = [code[:, h, :].bitcast(u32) for h in range(NH)]

        acc_plus = [bank(f"acc_plus{i}") for i in range(2)]
        acc_minus = [bank(f"acc_minus{i}") for i in range(2)]
        work = [bank(f"work{i}") for i in range(4)]
        s1_ps, s1b_ps, mean_ps = acc_plus[0], acc_plus[1], acc_minus[0]
        misc_ps = work[2]

        x_landed = [sem(f"x_landed{i}") for i in range(4)]
        w_landed = sem("w_landed")
        adj_landed = [sem(f"adj_landed{q}") for q in range(CH)]
        ident_ready = sem("ident_ready")
        ones_ready = sem("ones_ready")
        weights_step = sem("weights_step")
        pe_weights = sem("pe_weights")
        bound_root = sem("bound_root")
        stats_step = sem("stats_step")
        var_ready = sem("var_ready")
        root_ready = sem("root_ready")
        hn_ready = sem("hn_ready")
        turned = sem("turned")
        relu_done = sem("relu_done")
        s1_mm = sem("s1_mm")
        s1_copied = sem("s1_copied")
        s1b_mm = sem("s1b_mm")
        s1bias_ready = sem("s1bias_ready")
        s2_mm = sem("s2_mm")
        s2_copied = sem("s2_copied")
        s2_step = sem("s2_step")
        s2max_ready = sem("s2max_ready")
        bexp_ready = sem("bexp_ready")
        aexp_ready = sem("aexp_ready")
        mean_step = sem("mean_step")
        mean_mm = sem("mean_mm")
        h_mm = sem("h_mm")
        set_ready = sem("set_ready")
        uv32_ready = sem("uv32_ready")
        high_ready = sem("high_ready")
        low_ready = sem("low_ready")
        noedge_dve = sem("noedge_dve")
        noedge_act = sem("noedge_act")
        signs_ready = sem("signs_ready")
        code_ready = sem("code_ready")
        code_turned = sem("code_turned")
        masks_ready = sem("masks_ready")
        chunk_summed = sem("chunk_summed")
        pair_factors = sem("pair_factors")
        plus_scaled = sem("plus_scaled")
        both_added = sem("both_added")
        sums_ready = sem("sums_ready")
        finish_step = sem("finish_step")
        elu_exp = sem("elu_exp")
        xres_landed = sem("xres_landed")
        result_ready = sem("result_ready")
        result_stored = sem("result_stored")

        FINISH_STEPS = 10
        S_ACT = 1
        S_DVE = NS - S_ACT

        block = ctx.enter_context(nc.Block())


        def load_adj(eng, n, q, quarters):
            b = 2 * n + q // NH
            for g in quarters:
                eng.dma_start(raw_slot[q][32 * g:32 * g + 32, :, :],
                              adj_view[g, q % NH, :, b, :, :]).then_inc(adj_landed[q], 16)

        @block.sync
        def _(sp):
            sp.dma_start(w_sb[:, :], W).then_inc(w_landed, 16)
            for i in range(2):
                sp.dma_start(a_sb[:, i:i + 1], a[i * F:(i + 1) * F, :]).then_inc(w_landed, 16)
            for i in range(4):
                part = slice(i * NB // 4, (i + 1) * NB // 4)
                sp.dma_start(x_sb[:, part, :], x_tiles[:, part, :]).then_inc(x_landed[i], 16)
            load_adj(sp, 0, 0, (0, 1))
            load_adj(sp, 0, 1, (0, 1))
            sp.wait_ge(set_ready, G)
            load_adj(sp, 0, 2, (0, 1))
            load_adj(sp, 0, 3, (0, 1))
            sp.wait_ge(low_ready, 2 * G)
            sp.dma_start(xres[:, :, :], x_tiles[:, 0:2, :]).then_inc(xres_landed, 16)

            def load_iteration(n):
                for q in range(CH):
                    sp.wait_ge(noedge_dve, CH * n + q - CH + 1)
                    sp.wait_ge(noedge_act, CH * n + q - CH + 1)
                    load_adj(sp, n, q, (0, 1))

            load_iteration(1)
            with sp.Fori(2, NI) as n:
                load_iteration(n)
                sp.wait_ge(result_ready, n - 1)
                sp.dma_start(out_tiles[:, bass.ds(2 * n - 4, 2), :], result[:, :, :])\
                    .then_inc(result_stored, 16)
                sp.dma_start(xres[:, :, :], x_tiles[:, bass.ds(2 * n - 2, 2), :]).then_inc(xres_landed, 16)
            sp.wait_ge(result_ready, NI - 1)
            sp.dma_start(out_tiles[:, NB - 4:NB - 2, :], result[:, :, :]).then_inc(result_stored, 16)
            sp.dma_start(xres[:, :, :], x_tiles[:, NB - 2:NB, :]).then_inc(xres_landed, 16)
            sp.wait_ge(result_ready, NI)
            sp.dma_start(out_tiles[:, NB - 2:NB, :], result[:, :, :]).then_inc(result_stored, 16)
            sp.wait_ge(result_stored, 16 * NI)

        @block.gpsimd
        def _(pool):
            pool.memset(ident[:, :], 0.0).then_inc(ident_ready, 1)
            pool.wait_ge(ident_ready, 1)
            pool.affine_select(out=ident[:, :], in_=ident[:, :], compare_op=ALU.not_equal, fill=1.0,
                               base=0, pattern=[[-1, P]], channel_multiplier=1).then_inc(ident_ready, 1)
            pool.wait_ge(ident_ready, 2)
            for s in range(NS):
                for g in range(NQ):
                    pool.tensor_copy(sel[:, s, g, :], ident[:, 32 * s:32 * s + 32]).then_inc(ident_ready, 1)

            def low_parts(gr):
                pool.wait_ge(high_ready, 2 * gr + 2)
                for w in range(2):
                    lo = uv[:, NK * gr:NK * gr + NK, 2 * R * w + R:2 * R * w + R + F]
                    hi = uv[:, NK * gr:NK * gr + NK, 2 * R * w:2 * R * w + F]
                    pool.tensor_tensor(lo, uv32[:, gr % 2, w, :, :], hi, ALU.subtract).then_inc(low_ready, 1)

            by_set = hn_t.rearrange("f (g m b k) -> f m k g b", g=NQ, b=32, k=NK)
            pool.wait_ge(relu_done, 16)
            for gr in range(G):
                if gr >= 4:
                    pool.wait_ge(h_mm, gr - 3)
                for k in range(NK):
                    ins = pool.tensor_copy(hn_set[:, gr % 4, P * k:P * (k + 1)].rearrange("f (g b) -> f g b", g=NQ),
                                           by_set[:, gr, k, :, :])
                ins.then_inc(set_ready, 1)
                if gr == 3:
                    pool.wait_ge(s2_step, 1)
                    pool.partition_all_reduce(small[:, 1:2], small[:, 0:1], P, RMAX).then_inc(s2max_ready, 1)
                if gr >= 4:
                    low_parts(gr - 4)
            for gr in range(G - 4, G):
                low_parts(gr)

        @block.scalar
        def _(act):
            def chunk(n, q, load=None, first=False):
                c = CH * n + q
                h = q % NH
                if load is not None:
                    act.wait_ge(noedge_dve, c - 1)
                    act.wait_ge(noedge_act, c - 1)
                    load_adj(act, *load, (2, 3))
                act.wait_ge(adj_landed[q], 64 * n + 64)
                if not first:
                    act.wait_ge(code_turned, c - 1)
                act.activation(noedge[:, h, S_DVE * CC:].bitcast(dt.int8),
                               raw_slot[q][:, S_DVE:, :].rearrange("p s c -> p (s c)"),
                               ACT.Sign, scale=2.0, bias=small[:, 7:8]).then_inc(noedge_act, 1)
                for s in range(NS):
                    ins = act.activation(code[:, h, s * CC:(s + 1) * CC], s2row[:, h * CC:(h + 1) * CC],
                                         ACT.Sign, bias=s1bias_at(n, q, s))
                ins.then_inc(signs_ready, 1)

            def s1bias_at(n, q, s):
                b = 2 * n + q // NH
                return s1bias[:, bass.ds(b, 1), s:s + 1].rearrange("p b s -> p (b s)")

            def scale_plus(pair, par):
                act.wait_ge(chunk_summed, CH * pair + NH * par + NH)
                act.wait_ge(pair_factors, pair + 1)
                act.activation(scaled_plus[:, par, :], acc_plus[par][:, 0:2 * R], ACT.Copy,
                               scale=a_now[:, par:par + 1]).then_inc(plus_scaled, 1)

            def fetch_factors(pair):
                act.activation(a_now[:, :], a_plus[:, bass.ds(2 * pair, 2)], ACT.Copy)\
                    .then_inc(pair_factors, 1)

            def elu_exponential(pair):
                act.wait_ge(finish_step, FINISH_STEPS * pair + 8)
                act.activation(yexp[:, :, :], ymin[:, :, :], ACT.Exp).then_inc(elu_exp, 1)

            load_adj(act, 0, 0, (2, 3))
            load_adj(act, 0, 1, (2, 3))
            act.wait_ge(weights_step, 4)
            act.activation(small[:, 3:4], small[:, 2:3], ACT.Sqrt, scale=float(F)).then_inc(bound_root, 1)

            def root(i):
                part = slice(i * NB // 4, (i + 1) * NB // 4)
                act.wait_ge(var_ready, i + 1)
                act.activation(ln[:, 2, part], ln[:, 1, part], ACT.Sqrt).then_inc(root_ready, 1)

            def relu(i):
                for gr in range(4 * i, 4 * i + 4):
                    act.wait_ge(turned, gr + 1)
                    act.activation(hn_t[:, 4 * P * gr:4 * P * (gr + 1)], work[gr % 2][:, :], ACT.Relu,
                                   accum_out=colsum[:, gr:gr + 1]).then_inc(relu_done, 1)

            root(0)
            root(1)
            relu(0)
            root(2)
            relu(1)
            root(3)
            relu(2)
            relu(3)
            for i in range(4):
                act.wait_ge(s2_mm, i + 1)
                act.activation(s2row[:, 512 * i:512 * (i + 1)], work[i % 2][:, :], ACT.Copy).then_inc(s2_copied, 1)
            act.wait_ge(s2_step, 4)
            act.activation(bexp[:, 0, :], s2_turned[:, :, 0], ACT.Exp, bias=small[:, 4:5]).then_inc(bexp_ready, 1)
            act.activation(bexp[:, 1, :], s2_turned[:, :, 0], ACT.Exp, bias=small[:, 5:6],
                           scale=ALPHA).then_inc(bexp_ready, 1)
            act.wait_ge(s1bias_ready, 2)
            chunk(0, 0, first=True)

            def high_parts(groups):
                for gr in groups:
                    for w in range(2):
                        act.wait_ge(uv32_ready, 2 * gr + w + 1)
                        act.activation(uv[:, NK * gr:NK * gr + NK, 2 * R * w:2 * R * w + F],
                                       uv32[:, gr % 2, w, :, :], ACT.Copy).then_inc(high_ready, 1)

            high_parts(range(0, G // 2))
            chunk(0, 1, first=True)
            high_parts(range(G // 2, G))
            act.wait_ge(set_ready, G)
            load_adj(act, 0, 2, (2, 3))
            load_adj(act, 0, 3, (2, 3))
            act.wait_ge(s2_step, 7)
            act.activation(a_plus[:, :], zmax[:, 1, :], ACT.Exp).then_inc(aexp_ready, 1)
            act.activation(a_minus[:, :], zmax[:, 2, :], ACT.Exp).then_inc(aexp_ready, 1)
            act.wait_ge(aexp_ready, 2)
            chunk(0, 2, load=(1, 0))
            chunk(0, 3, load=(1, 1))
            chunk(1, 0, load=(1, 2))
            fetch_factors(0)
            scale_plus(0, 0)
            chunk(1, 1, load=(1, 3))
            chunk(1, 2, load=(2, 0))
            scale_plus(0, 1)
            chunk(1, 3, load=(2, 1))
            elu_exponential(0)

            def iteration(n, last=False):
                chunk(n, 0, load=(n, 2))
                fetch_factors(n - 1)
                scale_plus(n - 1, 0)
                chunk(n, 1, load=(n, 3))
                chunk(n, 2, load=None if last else (n + 1, 0))
                scale_plus(n - 1, 1)
                chunk(n, 3, load=None if last else (n + 1, 1))
                elu_exponential(n - 1)

            with act.Fori(2, NI - 1) as n:
                iteration(n)
            iteration(NI - 1, last=True)
            act.wait_ge(plus_scaled, NB - 2)
            fetch_factors(NI - 1)
            scale_plus(NI - 1, 0)
            scale_plus(NI - 1, 1)
            elu_exponential(NI - 1)

        @block.vector
        def _(dve):
            dve.memset(ones[:, :], 1.0).then_inc(ones_ready, 1)
            dve.memset(small[:, 7:8], -1.0).then_inc(s1bias_ready, 1)

            dve.wait_ge(w_landed, 48)
            dve.tensor_tensor(w_sq[:, :], w_sb[:, :], w_sb[:, :], ALU.mult).then_inc(weights_step, 1)
            dve.wait_ge(pe_weights, 1)
            dve.tensor_copy(w_t[:, :], misc_ps[:, 0:F]).then_inc(weights_step, 1)
            dve.wait_ge(pe_weights, 3)
            dve.tensor_copy(wa[:, :], misc_ps[:, 128:130]).then_inc(weights_step, 1)
            dve.reduce_max(small[:, 2:3], misc_ps[:, 256:256 + F], AX.X).then_inc(weights_step, 1)
            dve.wait_ge(weights_step, 4)
            dve.tensor_scalar(wa2_rep[:, :], ones[:, 0:32], wa[:, 1:2], None, ALU.mult).then_inc(weights_step, 1)
            dve.wait_ge(bound_root, 1)
            dve.tensor_scalar(h_bound[:, :], small[:, 3:4], 1e-30, None, ALU.max).then_inc(weights_step, 1)
            dve.wait_ge(weights_step, 6)
            dve.reciprocal(small[:, 6:7], h_bound[:, :]).then_inc(weights_step, 1)

            step = [0]

            def after(ins):
                step[0] += 1
                ins.then_inc(stats_step, 1)
                dve.wait_ge(stats_step, step[0])

            def variances(i):
                part = slice(i * NB // 4, (i + 1) * NB // 4)
                dve.wait_ge(x_landed[i], 16)
                for b in range(i * NB // 4, (i + 1) * NB // 4):
                    ins = dve.bn_stats(stats[:, b, :], x_sb[:, b, :])
                after(ins)
                mean_e, m2_e = stats[:, part, 1], stats[:, part, 2]
                mean_o, m2_o = stats[:, part, 4], stats[:, part, 5]
                dve.tensor_tensor(ln[:, 3, part], mean_e, mean_o, ALU.add)
                dve.tensor_tensor(ln[:, 4, part], mean_e, mean_o, ALU.subtract)
                after(dve.tensor_tensor(ln[:, 5, part], m2_e, m2_o, ALU.add))
                dve.tensor_scalar(ln[:, 0, part], ln[:, 3, part], 0.5, None, ALU.mult)
                dve.tensor_scalar(ln[:, 5, part], ln[:, 5, part], 1.0 / F, EPS, ALU.mult, ALU.add)
                after(dve.tensor_tensor(ln[:, 6, part], ln[:, 4, part], ln[:, 4, part], ALU.mult))
                dve.scalar_tensor_tensor(ln[:, 1, part], ln[:, 6, part], 0.25, ln[:, 5, part],
                                         ALU.mult, ALU.add).then_inc(var_ready, 1)

            def normalise(i):
                part = slice(i * NB // 4, (i + 1) * NB // 4)
                dve.wait_ge(root_ready, i + 1)
                after(dve.reciprocal(ln[:, 3, part], ln[:, 2, part]))
                after(dve.tensor_tensor(ln[:, 4, part], ln[:, 3, part], ln[:, 3, part], ALU.mult))
                after(dve.tensor_tensor(ln[:, 5, part], ln[:, 4, part], ln[:, 1, part], ALU.mult))
                after(dve.tensor_scalar(ln[:, 6, part], ln[:, 5, part], -0.5, 1.5, ALU.mult, ALU.add))
                after(dve.tensor_tensor(ln[:, 7, part], ln[:, 6, part], ln[:, 3, part], ALU.mult))
                for gr in range(4 * i, 4 * i + 4):
                    if gr >= 2:
                        dve.wait_ge(turned, gr - 1)
                    for k in range(4):
                        b = 4 * gr + k
                        ins = dve.tensor_scalar(hn[:, gr % 2, k, :], x_sb[:, b, :], ln[:, 0, b:b + 1],
                                                ln[:, 7, b:b + 1], ALU.subtract, ALU.mult)
                    ins.then_inc(hn_ready, 1)

            variances(0)
            variances(1)
            normalise(0)
            variances(2)
            normalise(1)
            variances(3)
            normalise(2)
            normalise(3)

            dve.wait_ge(relu_done, 16)
            dve.reduce_sum(colmean[:, :], colsum[:, :], AX.X).then_inc(mean_step, 1)
            dve.wait_ge(mean_step, 1)
            dve.tensor_scalar(colmean_rep[:, :], ones[:, :], colmean[:, :], 1.0 / N,
                              ALU.mult, ALU.mult).then_inc(mean_step, 1)
            dve.wait_ge(s1_mm, 1)
            dve.tensor_copy(s1col[:, :], s1_ps[:, 0:NB]).then_inc(s1_copied, 1)

            dve.wait_ge(s2_copied, 4)
            dve.reduce_max(small[:, 0:1], s2row[:, :], AX.X).then_inc(s2_step, 1)
            dve.wait_ge(s1b_mm, 1)
            dve.tensor_copy(s1bias[:, :, :].rearrange("p b s -> p s b"),
                            s1b_ps[:, 0:NS * NB].rearrange("p (s b) -> p s b", s=NS)).then_inc(s1bias_ready, 1)
            dve.transpose(s2_turned[:, :, :].rearrange("p (t k) a -> p t k a", k=NK),
                          s2row[:, :].rearrange("p (t b k) -> p t k b", b=32, k=NK)).then_inc(s2_step, 1)
            dve.wait_ge(s2max_ready, 1)
            dve.tensor_scalar(small[:, 4:5], small[:, 1:2], -1.0, None, ALU.mult).then_inc(s2_step, 1)
            dve.tensor_scalar(small[:, 5:6], small[:, 1:2], -ALPHA, None, ALU.mult).then_inc(s2_step, 1)

            dve.wait_ge(s1_copied, 1)
            dve.tensor_scalar(zmax[:, 0, :], s1col[:, :], small[:, 1:2], None, ALU.add).then_inc(s2_step, 1)
            dve.wait_ge(s2_step, 5)
            dve.tensor_scalar(zmax[:, 1, :], zmax[:, 0, :], 1.0 - ALPHA, 0.0, ALU.mult, ALU.min)\
                .then_inc(s2_step, 1)
            dve.tensor_scalar(zmax[:, 2, :], zmax[:, 0, :], ALPHA - 1.0, 0.0, ALU.mult, ALU.min)\
                .then_inc(s2_step, 1)
            dve.wait_ge(mean_mm, 1)
            dve.tensor_copy(mean_h[:, :], mean_ps[:, 0:F]).then_inc(mean_step, 1)

            dve.wait_ge(bexp_ready, 2)
            dve.wait_ge(weights_step, 7)
            for w in range(2):
                dve.tensor_scalar(bscaled[:, w, :], bexp[:, w, :], small[:, 6:7], FP16_TOP,
                                  ALU.mult, ALU.mult).then_inc(bexp_ready, 1)
                dve.tensor_scalar(uv[:, :, 2 * R * w + F], bexp[:, w, :], FP16_TOP, None,
                                  ALU.mult).then_inc(bexp_ready, 1)
            dve.wait_ge(bexp_ready, 6)
            for w in range(2):
                dve.scalar_tensor_tensor(uv[:, :, 2 * R * w + R + F], bexp[:, w, :], FP16_TOP,
                                         uv[:, :, 2 * R * w + F], ALU.mult, ALU.subtract).then_inc(bexp_ready, 1)

            def chunk(n, q, first=False):
                c = CH * n + q
                h = q % NH
                dve.wait_ge(adj_landed[q], 64 * n + 64)
                if not first:
                    dve.wait_ge(code_ready, c - 1)
                dve.tensor_scalar(noedge[:, h, 0:S_DVE * CC],
                                  raw_slot[q][:, 0:S_DVE, :].rearrange("p s c -> p (s c)"),
                                  0.0, float(NOEDGE), ALU.is_le, ALU.mult).then_inc(noedge_dve, 1)
                dve.wait_ge(noedge_dve, c + 1)
                dve.wait_ge(noedge_act, c + 1)
                dve.wait_ge(signs_ready, c + 1)
                dve.scalar_tensor_tensor(code_words[h], code_words[h], MINUS4, noedge_words[h],
                                         ALU.bitwise_xor, ALU.bitwise_or).then_inc(code_ready, 1)
                dve.wait_ge(code_ready, c + 1)
                if not first:
                    dve.wait_ge(chunk_summed, c - 1)
                dve.transpose(minus[:, h, :].rearrange("p (t s a) -> p s t a", s=NS, a=32),
                              code_words[h].rearrange("p (s t b) -> p s t b", s=NS, b=32))\
                    .then_inc(code_turned, 1)
                dve.wait_ge(code_turned, c + 1)
                dve.tensor_scalar(plus[:, h, :], minus[:, h, :], PLUS4, PLUS4,
                                  ALU.bitwise_and, ALU.bitwise_xor).then_inc(masks_ready, 1)
                dve.tensor_scalar(minus[:, h, :], minus[:, h, :], MINUS4, MINUS4,
                                  ALU.bitwise_and, ALU.bitwise_xor).then_inc(masks_ready, 1)

            def add_minus(b, par):
                dve.wait_ge(plus_scaled, b + 1)
                dve.scalar_tensor_tensor(both[:, par, :], acc_minus[par][:, 0:2 * R], a_minus[:, bass.ds(b, 1)],
                                         scaled_plus[:, par, :], ALU.mult, ALU.add).then_inc(both_added, 1)
                dve.wait_ge(both_added, b + 1)
                dve.tensor_tensor(sums[:, par, :], both[:, par, 0:R], both[:, par, R:2 * R],
                                  ALU.add).then_inc(sums_ready, 1)

            def finish(pair):
                base = FINISH_STEPS * pair
                dve.wait_ge(sums_ready, 2 * pair + 2)
                dve.tensor_scalar(empty[:, :], sums[:, :, F], 0.0, None, ALU.is_equal).then_inc(finish_step, 1)
                dve.scalar_tensor_tensor(den[:, :], sums[:, :, F], 0.0, sums[:, :, F],
                                         ALU.is_equal, ALU.add).then_inc(finish_step, 1)
                dve.wait_ge(finish_step, base + 2)
                dve.reciprocal(rden[:, :], den[:, :]).then_inc(finish_step, 1)
                dve.wait_ge(finish_step, base + 3)
                dve.tensor_scalar(rscale[:, :], rden[:, :], h_bound[:, :], None, ALU.mult).then_inc(finish_step, 1)
                dve.wait_ge(finish_step, base + 4)
                for par in range(2):
                    dve.tensor_scalar(fallback[:, par, :], mean_h[:, :], empty[:, par:par + 1], None,
                                      ALU.mult).then_inc(finish_step, 1)
                dve.wait_ge(finish_step, base + 6)
                for par in range(2):
                    ins = dve.scalar_tensor_tensor(y[:, par, :], sums[:, par, 0:F], rscale[:, par:par + 1],
                                                   fallback[:, par, :], ALU.mult, ALU.add)
                ins.then_inc(finish_step, 1)
                dve.wait_ge(finish_step, base + 7)
                dve.tensor_scalar(ymin[:, :, :], y[:, :, :], 0.0, None, ALU.min).then_inc(finish_step, 1)

            def finish_elu(pair):
                base = FINISH_STEPS * pair
                dve.wait_ge(elu_exp, pair + 1)
                dve.tensor_scalar(yexp[:, :, :], yexp[:, :, :], -1.0, None, ALU.add).then_inc(finish_step, 1)
                dve.wait_ge(finish_step, base + 9)
                dve.scalar_tensor_tensor(elu1[:, :, :], y[:, :, :], 0.0, yexp[:, :, :],
                                         ALU.max, ALU.add).then_inc(finish_step, 1)
                dve.wait_ge(finish_step, base + 10)
                dve.wait_ge(xres_landed, 16 * pair + 16)

            def put_result(pair, first=False):
                if not first:
                    dve.wait_ge(result_stored, 16 * pair)
                dve.tensor_tensor(result[:, :, :], elu1[:, :, :], xres[:, :, :], ALU.add)\
                    .then_inc(result_ready, 1)

            def scaled_factors(groups):
                for gr in groups:
                    dve.wait_ge(h_mm, gr + 1)
                    if gr >= 2:
                        dve.wait_ge(low_ready, 2 * gr - 2)
                    h4 = work[gr % 4][:, :].rearrange("p (k f) -> p k f", k=NK)
                    for w in range(2):
                        factor = bscaled[:, w, NK * gr:NK * gr + NK].rearrange("p (k o) -> p k o", o=1)\
                            .to_broadcast([P, NK, F])
                        dve.tensor_tensor(uv32[:, gr % 2, w, :, :], h4, factor, ALU.mult).then_inc(uv32_ready, 1)

            chunk(0, 0, first=True)
            scaled_factors(range(0, G // 2))
            chunk(0, 1, first=True)
            scaled_factors(range(G // 2, G))
            dve.wait_ge(aexp_ready, 2)
            dve.tensor_scalar(a_minus[:, :], a_minus[:, :], MINUS_RESCALE, None, ALU.mult).then_inc(aexp_ready, 1)
            chunk(0, 2)
            chunk(0, 3)
            dve.wait_ge(aexp_ready, 3)
            add_minus(0, 0)

            def iteration(n, first=False):
                chunk(n, 0)
                chunk(n, 1)
                add_minus(2 * n - 1, 1)
                finish(n - 1)
                chunk(n, 2)
                chunk(n, 3)
                finish_elu(n - 1)
                put_result(n - 1, first=first)
                add_minus(2 * n, 0)

            iteration(1, first=True)
            with dve.Fori(2, NI) as n:
                iteration(n)
            add_minus(NB - 1, 1)
            finish(NI - 1)
            finish_elu(NI - 1)
            put_result(NI - 1)

        @block.tensor
        def _(pe):
            pe.wait_ge(w_landed, 48)
            pe.wait_ge(ident_ready, 2)
            pe.transpose(misc_ps[:, 0:F], w_sb[:, :], ident[:, :]).then_inc(pe_weights, 1)
            pe.wait_ge(ones_ready, 1)
            pe.wait_ge(weights_step, 2)
            pe.matmul(misc_ps[:, 256:256 + F], ones[:, :], w_sq[:, :], start=True, stop=True)\
                .then_inc(pe_weights, 1)
            pe.matmul(misc_ps[:, 128:130], w_t[:, :], a_sb[:, :], start=True, stop=True).then_inc(pe_weights, 1)

            def s1_columns(gr):
                pe.wait_ge(relu_done, gr + 1)
                for b in range(4 * gr, 4 * gr + 4):
                    ins = pe.matmul(s1_ps[:, b:b + 1], hn_t[:, P * b:P * (b + 1)], wa[:, 0:1],
                                    start=True, stop=True)
                return ins

            for gr in range(16):
                pe.wait_ge(hn_ready, gr + 1)
                if gr >= 2:
                    pe.wait_ge(relu_done, gr - 1)
                for k in range(4):
                    ins = pe.transpose(work[gr % 2][:, P * k:P * (k + 1)], hn[:, gr % 2, k, :], ident[:, :])
                ins.then_inc(turned, 1)
                if gr == 0:
                    pe.wait_ge(weights_step, 5)
                else:
                    s1_columns(gr - 1)
            s1_columns(15).then_inc(s1_mm, 1)
            for i in range(4):
                if i >= 2:
                    pe.wait_ge(s2_copied, i - 1)
                for g in range(NQ):
                    ins = pe.matmul(work[i % 2][32 * g:32 * g + 32, :], wa2_rep[:, :],
                                    hn_t[:, QC * g + 512 * i:QC * g + 512 * (i + 1)], start=True, stop=True)
                ins.then_inc(s2_mm, 1)
            pe.wait_ge(s1_copied, 1)
            pe.wait_ge(ident_ready, 2 + NS * NQ)
            for s in range(NS):
                ins = pe.matmul(s1b_ps[:, NB * s:NB * (s + 1)], sel[:, s, :, :].rearrange("p g b -> p (g b)"),
                                s1col[:, :], start=True, stop=True)
            ins.then_inc(s1b_mm, 1)
            pe.wait_ge(mean_step, 2)
            pe.matmul(mean_ps[:, 0:F], colmean_rep[:, :], w_sb[:, :], start=True, stop=True).then_inc(mean_mm, 1)
            pe.wait_ge(s2_copied, 4)

            def h_group(gr):
                pe.wait_ge(set_ready, gr + 1)
                if gr >= 4:
                    pe.wait_ge(uv32_ready, 2 * gr - 6)
                for k in range(NK):
                    ins = pe.matmul(work[gr % 4][:, P * k:P * (k + 1)], hn_set[:, gr % 4, P * k:P * (k + 1)],
                                    w_sb[:, :], start=True, stop=True)
                ins.then_inc(h_mm, 1)

            for gr in range(G):
                h_group(gr)

            plus8 = [plus[:, h, :].bitcast(dt.float8e4).rearrange("p (t i k) -> p t k i", t=NT, k=NK)
                     for h in range(NH)]
            minus8 = [minus[:, h, :].bitcast(dt.float8e4).rearrange("p (t i k) -> p t k i", t=NT, k=NK)
                      for h in range(NH)]

            def chunk(n, q, first=False):
                h, par = q % NH, q // NH
                pe.wait_ge(masks_ready, 2 * CH * n + 2 * q + 2)
                pe.ldweights(uv[:, 0, 0:P], tile_position=(0, 0))
                for t in range(NT):
                    if first:
                        pe.wait_ge(low_ready, 2 * (NT * h + t) + 2)
                    for k in range(NK):
                        j = (NT * h + t) * NK + k
                        ends = dict(start=(j == 0), stop=(j == NJ - 1))
                        pe.matmul(acc_plus[par][:, 0:2 * R], plus8[h][:, t, k, :], uv[:, j, 0:2 * R], **ends)
                        ins = pe.matmul(acc_minus[par][:, 0:2 * R], minus8[h][:, t, k, :],
                                        uv[:, j, 2 * R:4 * R], **ends)
                ins.then_inc(chunk_summed, 1)

            pe.wait_ge(bexp_ready, 8)
            pe.wait_ge(s1bias_ready, 2)
            pe.wait_ge(mean_step, 3)
            for q in range(CH):
                chunk(0, q, first=q < NH)
            with pe.Fori(1, NI) as n:
                for q in range(CH):
                    if q % NH == 0:
                        pe.wait_ge(both_added, 2 * n + q // NH - 1)
                    chunk(n, q)


_INS = ['x', 'adj', 'L0_gnn_W', 'L0_gnn_a']


def kernel(**inputs):
    import numpy as _np
    import concourse.bacc as _bacc
    from concourse.bass_utils import run_bass_kernel_spmd as _run

    nc = _bacc.Bacc("TRN2", target_bir_lowering=False, num_devices=1)
    arrays, args = {}, []
    for name in _INS:
        arr = _np.ascontiguousarray(inputs[name])
        arrays[f"in_{name}_dram"] = arr
        args.append(nc.dram_tensor(f"in_{name}_dram", arr.shape, mybir.dt.from_np(arr.dtype),
                                   kind="ExternalInput").ap())
    args.append(nc.dram_tensor("out_dram", tuple(inputs['x'].shape), dt.float32, kind="ExternalOutput").ap())
    build(nc, *args)
    r = _run(nc, [arrays], core_ids=[0])
    return r.results[0]["out_dram"]
```

```python
import concourse.bass as bass
from concourse import mybir
from contextlib import ExitStack

dt = mybir.dt
ALU = mybir.AluOpType
ACT = mybir.ActivationFunctionType
AX = mybir.AxisListType
RMAX = bass.bass_isa.ReduceOp.max

ALPHA = 0.2
EPS = 1e-5

PLUS, MINUS = 0x20, 0x10
NOEDGE = PLUS | MINUS
PLUS4, MINUS4 = PLUS * 0x01010101, MINUS * 0x01010101
MINUS_RESCALE = 4.0
FP16_TOP = 32768.0


def build(nc, x, adj, W, a, out):
    N, F = x.shape
    P = 128
    NB = N // P
    NQ = 4
    QC = N // NQ
    NH = 2
    CC = QC // NH
    NS = 4
    NT = CC // 128
    NK = 4
    NJ = NH * NT * NK
    NI = NB // 2
    CH = 2 * NH
    R = F + 1
    CW = CC // 4
    G = NJ // NK
    XP = 4
    GP = G // XP
    f32, f16, u32 = dt.float32, dt.float16, dt.uint32

    x_tiles = x.rearrange("(b p) f -> p b f", p=P)
    x_quarters = x.rearrange("(g m p) f -> g p m f", g=NQ, p=P)
    out_tiles = out.rearrange("(b p) f -> p b f", p=P)
    adj_view = adj.rearrange("(b s a) (g h c) -> g h a b s c", s=NS, a=32, g=NQ, h=NH)

    ctx = ExitStack()
    with ctx:
        def sb(name, shape, d):
            return ctx.enter_context(nc.sbuf_tensor(name, shape, d))

        def bank(name):
            return ctx.enter_context(nc.psum_tensor(name, [P, 512], f32))

        def sem(name):
            return ctx.enter_context(nc.semaphore(name))

        raw = sb("raw", [P, CH * NS * CC], dt.int32)
        noedge = sb("noedge", [P, NH, NS * CC], dt.uint8)
        code = sb("code", [P, NH, NS * CC], dt.int8)
        minus = sb("minus", [P, NH, NS * CW], u32)
        plus = sb("plus", [P, NH, NS * CW], u32)
        uv = sb("uv", [P, NJ, 4 * R], f16)
        s2row = sb("s2row", [P, QC], f32)
        s1bias = sb("s1bias", [P, NB, NS], f32)
        a_plus = sb("a_plus", [P, NB], f32)
        a_now = sb("a_now", [P, 2], f32)
        a_minus = sb("a_minus", [P, NB], f32)
        h_bound = sb("h_bound", [P, 1], f32)
        mean_h = sb("mean_h", [P, F], f32)
        scaled_plus = sb("scaled_plus", [P, 2, 2 * R], f32)
        both = sb("both", [P, 2, 2 * R], f32)
        sums = sb("sums", [P, 2, R], f32)
        empty = sb("empty", [P, 2], f32)
        den = sb("den", [P, 2], f32)
        rden = sb("rden", [P, 2], f32)
        rscale = sb("rscale", [P, 2], f32)
        ident = sb("ident", [P, P], f32)
        ones = sb("ones", [P, P], f32)
        w_sb = sb("w_sb", [P, F], f32)
        w_t = sb("w_t", [P, F], f32)
        w_sq = sb("w_sq", [P, F], f32)
        a_sb = sb("a_sb", [P, 2], f32)
        wa2_rep = sb("wa2_rep", [P, 32], f32)
        colsum = sb("colsum", [P, G], f32)
        colmean = sb("colmean", [P, 1], f32)
        colmean_rep = sb("colmean_rep", [P, P], f32)
        s1col = sb("s1col", [P, NB], f32)
        small = sb("small", [P, 12], f32)
        wa1_row = sb("wa1_row", [P, F], f32)
        a1_rep = sb("a1_rep", [P, P], f32)
        hn_t_high = sb("hn_t_high", [P, G // 2, NK * P], f32)
        bexp = sb("bexp", [P, 2, NJ], f32)
        bscaled = sb("bscaled", [P, 2, NJ], f32)
        zmax = sb("zmax", [P, 3, NB], f32)
        hn = sb("hn", [P, 4, NQ, F], f32)

        slot_words = NS * CC
        raw_slot = [raw[:, q * slot_words:(q + 1) * slot_words].rearrange("p (s c) -> p s c", s=NS)
                    for q in range(CH)]
        uv_flat = uv[:, :, :].rearrange("p j c -> p (j c)")
        x_sb = uv_flat[:, 0:2 * NB * F].bitcast(f32).rearrange("p (m g f) -> p m g f", g=NQ, f=F)
        low_start = 3 * NJ // 4 * 4 * R
        hn_t_low = uv_flat[:, low_start:low_start + N].bitcast(f32).rearrange("p (m n) -> p m n", n=NK * P)
        hn_t = [hn_t_low[:, m, :] for m in range(G // 2)] + [hn_t_high[:, m, :] for m in range(G // 2)]
        uv32 = hn[:, :, :, :].rearrange("p (i w) k f -> p i w k f", w=2)
        fallback, y, ymin, yexp, elu1, xres, result = [
            hn[:, i // 2, 2 * (i % 2):2 * (i % 2) + 2, :] for i in range(7)]
        early = minus[:, :, :].rearrange("p i c -> p (i c)").bitcast(f32)
        s1_terms = early[:, 0:NQ * F].rearrange("p (g f) -> p g f", f=F)
        sel = early[:, NQ * F:2 * NQ * F].rearrange("p (s g a) -> p s g a", s=NS, g=NQ)
        ln = early[:, 2 * NQ * F:2 * NQ * F + 8 * NB].rearrange("p (i b) -> p i b", b=NB)
        stats = early[:, 2 * NQ * F + 8 * NB:2 * NQ * F + 14 * NB].rearrange("p (b i) -> p b i", i=6)
        between = uv_flat[:, low_start - 2 * N // 4:low_start].bitcast(f32)
        s1_half = between[:, 0:NQ * 64].rearrange("p (g f) -> p g f", f=64)
        s1_product = between[:, NQ * 64:NQ * 64 + F]
        s1_folded = between[:, N // 8:N // 4].rearrange("p (m g f) -> p m g f", g=NQ, f=32)
        s2_turned = plus[:, :, :].rearrange("p h c -> p (h c)").bitcast(f32)\
            .rearrange("p (j a) -> p j a", a=32)
        noedge_words = [noedge[:, h, :].bitcast(u32) for h in range(NH)]
        code_words = [code[:, h, :].bitcast(u32) for h in range(NH)]

        acc_plus = [bank(f"acc_plus{i}") for i in range(2)]
        acc_minus = [bank(f"acc_minus{i}") for i in range(2)]
        work = [bank(f"work{i}") for i in range(4)]
        s2_ps = acc_plus
        s1b_ps = acc_minus[0][:, 0:NS * NB]
        mean_ps = acc_minus[0][:, NS * NB:NS * NB + F]
        misc_ps = acc_minus[1]

        x_landed = [sem(f"x_landed{i}") for i in range(XP)]
        w_landed = sem("w_landed")
        adj_landed = [sem(f"adj_landed{q}") for q in range(CH)]
        ident_ready = sem("ident_ready")
        ones_ready = sem("ones_ready")
        weights_step = sem("weights_step")
        pe_weights = sem("pe_weights")
        bound_root = sem("bound_root")
        stats_step = sem("stats_step")
        var_ready = sem("var_ready")
        root_ready = sem("root_ready")
        hn_ready = sem("hn_ready")
        turned = sem("turned")
        evac_dve = sem("evac_dve")
        evac_act = sem("evac_act")
        s1_step = sem("s1_step")
        s1_product_done = sem("s1_product_done")
        s1_summed = sem("s1_summed")
        s1b_mm = sem("s1b_mm")
        s1bias_ready = sem("s1bias_ready")
        s2_mm = sem("s2_mm")
        s2_copied = sem("s2_copied")
        s2_step = sem("s2_step")
        s2max_ready = sem("s2max_ready")
        bexp_ready = sem("bexp_ready")
        aexp_ready = sem("aexp_ready")
        mean_step = sem("mean_step")
        mean_mm = sem("mean_mm")
        rstd_ready = sem("rstd_ready")
        s2_part = sem("s2_part")
        bscaled_ready = sem("bscaled_ready")
        den_ready = sem("den_ready")
        h_mm = sem("h_mm")
        uv32_ready = sem("uv32_ready")
        high_ready = sem("high_ready")
        low_pool = sem("low_pool")
        low_dve = sem("low_dve")
        noedge_dve = sem("noedge_dve")
        noedge_act = sem("noedge_act")
        signs_ready = sem("signs_ready")
        code_ready = sem("code_ready")
        code_turned = sem("code_turned")
        masks_ready = sem("masks_ready")
        chunk_summed = sem("chunk_summed")
        pair_factors = sem("pair_factors")
        plus_scaled = sem("plus_scaled")
        both_added = sem("both_added")
        sums_ready = sem("sums_ready")
        finish_step = sem("finish_step")
        elu_exp = sem("elu_exp")
        xres_landed = sem("xres_landed")
        result_ready = sem("result_ready")
        result_stored = sem("result_stored")

        FINISH_STEPS = 10
        S_ACT = 1
        S_DVE = NS - S_ACT

        block = ctx.enter_context(nc.Block())


        def parity(n, q):
            return q % 2 if isinstance(n, int) and n == 0 else q // NH

        def half(n, q):
            return q // 2 if isinstance(n, int) and n == 0 else q % NH

        def load_adj(eng, n, q, quarters):
            for g in quarters:
                eng.dma_start(raw_slot[q][32 * g:32 * g + 32, :, :],
                              adj_view[g, half(n, q), :, 2 * n + parity(n, q), :, :]).then_inc(adj_landed[q], 16)

        def load_x(eng, i, quarters):
            for g in quarters:
                eng.dma_start(x_sb[:, GP * i:GP * (i + 1), g, :], x_quarters[g, :, GP * i:GP * (i + 1), :])\
                    .then_inc(x_landed[i], 16)

        def by_set(group):
            return group.rearrange("f (k g b) -> f k g b", k=NK, g=NQ)

        def by_node(bank_):
            return bank_[:, :].rearrange("f (g b k) -> f k g b", g=NQ, k=NK)

        def lows_pool(gr):
            return gr + 1 + (gr + 1) // 2

        def lows_dve(gr):
            return gr // 2 + 1

        def low_part(eng, gr, w):
            lo = uv[:, NK * gr:NK * gr + NK, 2 * R * w + R:2 * R * w + R + F]
            hi = uv[:, NK * gr:NK * gr + NK, 2 * R * w:2 * R * w + F]
            return eng.tensor_tensor(lo, uv32[:, gr % 2, w, :, :], hi, ALU.subtract)

        @block.sync
        def _(sp):
            sp.dma_start(w_sb[:, :], W).then_inc(w_landed, 16)
            for i in range(2):
                sp.dma_start(a_sb[:, i:i + 1], a[i * F:(i + 1) * F, :]).then_inc(w_landed, 16)
            for i in range(XP):
                load_x(sp, i, range(NQ))
            for q in range(CH):
                load_adj(sp, 0, q, range(NQ))

            def load_iteration(n):
                for q in range(CH):
                    sp.wait_ge(noedge_dve, CH * n + q - CH + 1)
                    sp.wait_ge(noedge_act, CH * n + q - CH + 1)
                    load_adj(sp, n, q, (0, 1))

            load_iteration(1)
            sp.wait_ge(low_pool, lows_pool(G - 1))
            sp.wait_ge(low_dve, lows_dve(G - 1))
            sp.dma_start(xres[:, :, :], x_tiles[:, 0:2, :]).then_inc(xres_landed, 16)
            with sp.Fori(2, NI) as n:
                load_iteration(n)
                sp.wait_ge(result_ready, n - 1)
                sp.dma_start(out_tiles[:, bass.ds(2 * n - 4, 2), :], result[:, :, :])\
                    .then_inc(result_stored, 16)
                sp.dma_start(xres[:, :, :], x_tiles[:, bass.ds(2 * n - 2, 2), :]).then_inc(xres_landed, 16)
            sp.wait_ge(result_ready, NI - 1)
            sp.dma_start(out_tiles[:, NB - 4:NB - 2, :], result[:, :, :]).then_inc(result_stored, 16)
            sp.dma_start(xres[:, :, :], x_tiles[:, NB - 2:NB, :]).then_inc(xres_landed, 16)
            sp.wait_ge(result_ready, NI)
            sp.dma_start(out_tiles[:, NB - 2:NB, :], result[:, :, :]).then_inc(result_stored, 16)
            sp.wait_ge(result_stored, 16 * NI)

        @block.gpsimd
        def _(pool):
            pool.memset(ident[:, :], 0.0).then_inc(ident_ready, 1)
            pool.wait_ge(ident_ready, 1)
            pool.affine_select(out=ident[:, :], in_=ident[:, :], compare_op=ALU.not_equal, fill=1.0,
                               base=0, pattern=[[-1, P]], channel_multiplier=1).then_inc(ident_ready, 1)
            pool.wait_ge(ident_ready, 2)
            for s in range(NS):
                for g in range(NQ):
                    pool.tensor_copy(sel[:, s, g, :], ident[:, 32 * s:32 * s + 32]).then_inc(ident_ready, 1)

            pool.wait_ge(weights_step, 6)
            row = wa1_row[:, :].rearrange("p (o f) -> p o f", o=1).to_broadcast([P, NQ, F])
            for i in range(G // 2):
                gr = 2 * i + 1
                pool.wait_ge(hn_ready, gr + 1)
                if i:
                    pool.wait_ge(s1_step, 3 * i)
                pool.tensor_tensor(s1_terms[:, :, :], hn[:, gr % 4, :, :], row, ALU.mult).then_inc(s1_step, 1)
                pool.wait_ge(s1_step, 3 * i + 1)
                pool.tensor_tensor(s1_half[:, :, :], s1_terms[:, :, 0:64], s1_terms[:, :, 64:128], ALU.add)\
                    .then_inc(s1_step, 1)
                pool.wait_ge(s1_step, 3 * i + 2)
                pool.tensor_tensor(s1_folded[:, i, :, :], s1_half[:, :, 0:32], s1_half[:, :, 32:64], ALU.add)\
                    .then_inc(s1_step, 1)
            pool.wait_ge(s2_step, 1)
            pool.partition_all_reduce(small[:, 1:2], small[:, 0:1], P, RMAX).then_inc(s2max_ready, 1)
            for gr in range(G):
                for w in range(1 + gr % 2):
                    pool.wait_ge(high_ready, 2 * gr + w + 1)
                    low_part(pool, gr, w).then_inc(low_pool, 1)

        @block.scalar
        def _(act):
            def edge_bytes(n, q, load=None, first=False):
                c = CH * n + q
                slot = q % 2
                if load is not None:
                    act.wait_ge(noedge_dve, c - 1)
                    act.wait_ge(noedge_act, c - 1)
                    load_adj(act, *load, (2, 3))
                act.wait_ge(adj_landed[q], 64 * n + 64)
                if not first:
                    act.wait_ge(code_turned, c - 1)
                act.activation(noedge[:, slot, S_DVE * CC:].bitcast(dt.int8),
                               raw_slot[q][:, S_DVE:, :].rearrange("p s c -> p (s c)"),
                               ACT.Sign, scale=2.0, bias=small[:, 7:8]).then_inc(noedge_act, 1)

            def signs(n, q, groups):
                h, slot = half(n, q), q % 2
                for s in groups:
                    act.activation(code[:, slot, s * CC:(s + 1) * CC], s2row[:, h * CC:(h + 1) * CC],
                                   ACT.Sign, bias=s1bias_at(n, q, s)).then_inc(signs_ready, 1)

            def chunk(n, q, load=None):
                edge_bytes(n, q, load)
                signs(n, q, range(NS))

            def s1bias_at(n, q, s):
                b = 2 * n + parity(n, q)
                return s1bias[:, bass.ds(b, 1), s:s + 1].rearrange("p b s -> p (b s)")

            def scale_plus(pair, par):
                first = isinstance(pair, int) and pair == 0
                act.wait_ge(chunk_summed, CH * pair + (3 + par if first else NH * par + NH))
                act.wait_ge(pair_factors, pair + 1)
                act.activation(scaled_plus[:, par, :], acc_plus[par][:, 0:2 * R], ACT.Copy,
                               scale=a_now[:, par:par + 1]).then_inc(plus_scaled, 1)

            def fetch_factors(pair):
                act.activation(a_now[:, :], a_plus[:, bass.ds(2 * pair, 2)], ACT.Copy)\
                    .then_inc(pair_factors, 1)

            def elu_exponential(pair):
                act.wait_ge(finish_step, FINISH_STEPS * pair + 8)
                act.activation(yexp[:, :, :], ymin[:, :, :], ACT.Exp).then_inc(elu_exp, 1)

            def root(i):
                part = slice(i * NB // XP, (i + 1) * NB // XP)
                act.wait_ge(var_ready, i + 1)
                act.activation(ln[:, 2, part], ln[:, 1, part], ACT.Sqrt).then_inc(root_ready, 1)

            def normalise(gr):
                act.wait_ge(rstd_ready, gr // GP + 1)
                if gr >= 4:
                    act.wait_ge(turned, gr - 3)
                    if gr % 2:
                        act.wait_ge(s1_step, 3 * (gr // 2 - 2) + 1)
                    else:
                        act.wait_ge(s1_product_done, 2 * gr - 4)
                for g in range(NQ):
                    b = NQ * gr + g
                    ins = act.activation(hn[:, gr % 4, g, :], x_sb[:, gr, g, :], ACT.Relu,
                                         scale=ln[:, 7, b:b + 1], bias=ln[:, 3, b:b + 1])
                ins.then_inc(hn_ready, 1)

            def evacuate(gr):
                act.wait_ge(turned, gr + 1)
                act.activation(by_set(hn_t[gr]), by_node(work[gr % 4]), ACT.Copy,
                               accum_out=colsum[:, gr:gr + 1]).then_inc(evac_act, 1)

            def s2_rows(i):
                act.wait_ge(s2_mm, i + 1)
                act.activation(s2row[:, 512 * i:512 * (i + 1)].rearrange("p (m b k) -> p m k b", k=NK, b=32),
                               s2_ps[i % 2][:, :].rearrange("p (m k b) -> p m k b", k=NK, b=32),
                               ACT.Copy).then_inc(s2_copied, 1)

            root(0)
            act.wait_ge(weights_step, 5)
            act.activation(small[:, 3:4], small[:, 2:3], ACT.Sqrt, scale=float(F)).then_inc(bound_root, 1)
            for gr in range(G):
                normalise(gr)
                if gr % GP == GP - 2 and gr // GP + 1 < XP:
                    root(gr // GP + 1)
                if gr >= 2 and gr % 2:
                    evacuate(gr - 2)
                if gr in (9, 13):
                    s2_rows(gr // 4 - 2)
            evacuate(G - 1)
            s2_rows(2)
            s2_rows(3)

            def high_parts(gr):
                for w in range(2):
                    act.wait_ge(uv32_ready, 2 * gr + w + 1)
                    act.activation(uv[:, NK * gr:NK * gr + NK, 2 * R * w:2 * R * w + F],
                                   uv32[:, gr % 2, w, :, :], ACT.Copy).then_inc(high_ready, 1)

            act.wait_ge(s1bias_ready, 1)
            edge_bytes(0, 0, first=True)
            act.wait_ge(s2_copied, 4)
            act.wait_ge(s1bias_ready, 2)
            signs(0, 0, (0, 1))
            act.wait_ge(s2_step, 3)
            act.activation(bexp[:, 0, :], s2_turned[:, :, 0], ACT.Exp, bias=small[:, 4:5]).then_inc(bexp_ready, 1)
            act.activation(bexp[:, 1, :], s2_turned[:, :, 0], ACT.Exp, bias=small[:, 5:6],
                           scale=ALPHA).then_inc(bexp_ready, 1)
            high_parts(0)
            signs(0, 0, (2, 3))
            high_parts(1)
            edge_bytes(0, 1, first=True)
            signs(0, 1, (0,))
            high_parts(2)
            signs(0, 1, (1, 2))
            high_parts(3)
            signs(0, 1, (3,))
            high_parts(4)
            high_parts(5)
            edge_bytes(0, 2, load=(1, 0))
            signs(0, 2, (0,))
            high_parts(6)
            signs(0, 2, (1, 2, 3))
            high_parts(7)
            high_parts(8)
            edge_bytes(0, 3, load=(1, 1))
            signs(0, 3, (0,))
            high_parts(9)
            signs(0, 3, (1, 2))
            high_parts(10)
            signs(0, 3, (3,))
            act.wait_ge(s2_step, 6)
            act.activation(a_plus[:, :], zmax[:, 1, :], ACT.Exp).then_inc(aexp_ready, 1)
            act.activation(a_minus[:, :], zmax[:, 2, :], ACT.Exp).then_inc(aexp_ready, 1)
            high_parts(11)
            high_parts(12)
            edge_bytes(1, 0, load=(1, 2))
            signs(1, 0, (0,))
            high_parts(13)
            signs(1, 0, (1, 2))
            high_parts(14)
            signs(1, 0, (3,))
            high_parts(15)
            chunk(1, 1, load=(1, 3))
            fetch_factors(0)
            scale_plus(0, 0)
            scale_plus(0, 1)
            chunk(1, 2, load=(2, 0))
            chunk(1, 3, load=(2, 1))
            elu_exponential(0)

            def iteration(n, last=False):
                chunk(n, 0, load=(n, 2))
                fetch_factors(n - 1)
                scale_plus(n - 1, 0)
                chunk(n, 1, load=(n, 3))
                chunk(n, 2, load=None if last else (n + 1, 0))
                scale_plus(n - 1, 1)
                chunk(n, 3, load=None if last else (n + 1, 1))
                elu_exponential(n - 1)

            with act.Fori(2, NI - 1) as n:
                iteration(n)
            iteration(NI - 1, last=True)
            act.wait_ge(plus_scaled, NB - 2)
            fetch_factors(NI - 1)
            scale_plus(NI - 1, 0)
            scale_plus(NI - 1, 1)
            elu_exponential(NI - 1)

        @block.vector
        def _(dve):
            dve.memset(ones[:, :], 1.0).then_inc(ones_ready, 1)
            dve.memset(small[:, 7:8], -1.0).then_inc(s1bias_ready, 1)

            step = [0]

            def after(ins):
                step[0] += 1
                ins.then_inc(stats_step, 1)
                dve.wait_ge(stats_step, step[0])

            def variances(i):
                part = slice(i * NB // XP, (i + 1) * NB // XP)
                dve.wait_ge(x_landed[i], 16 * NQ)
                for b in range(i * NB // XP, (i + 1) * NB // XP):
                    ins = dve.bn_stats(stats[:, b, :], x_sb[:, b // NQ, b % NQ, :])
                after(ins)
                mean_e, m2_e = stats[:, part, 1], stats[:, part, 2]
                mean_o, m2_o = stats[:, part, 4], stats[:, part, 5]
                dve.tensor_tensor(ln[:, 3, part], mean_e, mean_o, ALU.add)
                dve.tensor_tensor(ln[:, 4, part], mean_e, mean_o, ALU.subtract)
                after(dve.tensor_tensor(ln[:, 5, part], m2_e, m2_o, ALU.add))
                dve.tensor_scalar(ln[:, 0, part], ln[:, 3, part], 0.5, None, ALU.mult)
                dve.tensor_scalar(ln[:, 5, part], ln[:, 5, part], 1.0 / F, EPS, ALU.mult, ALU.add)
                after(dve.tensor_tensor(ln[:, 6, part], ln[:, 4, part], ln[:, 4, part], ALU.mult))
                dve.scalar_tensor_tensor(ln[:, 1, part], ln[:, 6, part], 0.25, ln[:, 5, part],
                                         ALU.mult, ALU.add).then_inc(var_ready, 1)

            def inverse_roots(i):
                part = slice(i * NB // XP, (i + 1) * NB // XP)
                dve.wait_ge(root_ready, i + 1)
                after(dve.reciprocal(ln[:, 3, part], ln[:, 2, part]))
                after(dve.tensor_tensor(ln[:, 4, part], ln[:, 3, part], ln[:, 3, part], ALU.mult))
                after(dve.tensor_tensor(ln[:, 5, part], ln[:, 4, part], ln[:, 1, part], ALU.mult))
                after(dve.tensor_scalar(ln[:, 6, part], ln[:, 5, part], -0.5, 1.5, ALU.mult, ALU.add))
                after(dve.tensor_tensor(ln[:, 7, part], ln[:, 6, part], ln[:, 3, part], ALU.mult))
                dve.scalar_tensor_tensor(ln[:, 3, part], ln[:, 0, part], -1.0, ln[:, 7, part],
                                         ALU.mult, ALU.mult).then_inc(rstd_ready, 1)

            def evacuate(groups):
                for gr in groups:
                    dve.wait_ge(turned, gr + 1)
                    dve.tensor_scalar(by_set(hn_t[gr]), by_node(work[gr % 4]), 0.0, None, ALU.max, ALU.add,
                                      accum_out=colsum[:, gr:gr + 1]).then_inc(evac_dve, 1)

            def weights():
                dve.wait_ge(w_landed, 48)
                dve.tensor_tensor(w_sq[:, :], w_sb[:, :], w_sb[:, :], ALU.mult).then_inc(weights_step, 1)
                dve.wait_ge(ones_ready, 1)
                dve.tensor_scalar(a1_rep[:, :], ones[:, :], a_sb[:, 0:1], None, ALU.mult).then_inc(weights_step, 1)
                dve.wait_ge(pe_weights, 1)
                dve.tensor_copy(w_t[:, :], misc_ps[:, 0:F]).then_inc(weights_step, 1)
                dve.wait_ge(pe_weights, 4)
                dve.tensor_scalar(wa2_rep[:, :], ones[:, 0:32], misc_ps[:, 128:129], None, ALU.mult)\
                    .then_inc(weights_step, 1)
                dve.reduce_max(small[:, 2:3], misc_ps[:, 256:256 + F], AX.X).then_inc(weights_step, 1)
                dve.tensor_copy(wa1_row[:, :], misc_ps[:, 384:384 + F]).then_inc(weights_step, 1)

            def bound():
                dve.wait_ge(bound_root, 1)
                dve.tensor_scalar(h_bound[:, :], small[:, 3:4], 1e-30, None, ALU.max).then_inc(weights_step, 1)
                dve.wait_ge(weights_step, 7)
                dve.reciprocal(small[:, 6:7], h_bound[:, :]).then_inc(weights_step, 1)

            def s1_of(gr):
                dve.wait_ge(hn_ready, gr + 1)
                for g in range(NQ):
                    if gr or g:
                        dve.wait_ge(s1_product_done, 2 * gr + g)
                    b = G * g + gr
                    dve.tensor_tensor_reduce(out=s1_product, in0=hn[:, gr % 4, g, :], in1=wa1_row[:, :],
                                             scale=1.0, scalar=0.0, op0=ALU.mult, op1=ALU.add,
                                             accum_out=s1col[:, b:b + 1]).then_inc(s1_product_done, 1)

            def denominators(h):
                sets = slice(NJ // NH * h, NJ // NH * (h + 1))
                for w in range(2):
                    dve.tensor_scalar(uv[:, sets, 2 * R * w + F], bexp[:, w, sets], FP16_TOP, None,
                                      ALU.mult).then_inc(den_ready, 1)
                dve.wait_ge(den_ready, 4 * h + 2)
                for w in range(2):
                    dve.scalar_tensor_tensor(uv[:, sets, 2 * R * w + R + F], bexp[:, w, sets], FP16_TOP,
                                             uv[:, sets, 2 * R * w + F], ALU.mult, ALU.subtract)\
                        .then_inc(den_ready, 1)

            def constants():
                dve.tensor_scalar(zmax[:, 1, :], zmax[:, 0, :], 1.0 - ALPHA, 0.0, ALU.mult, ALU.min)\
                    .then_inc(s2_step, 1)
                dve.tensor_scalar(zmax[:, 2, :], zmax[:, 0, :], ALPHA - 1.0, 0.0, ALU.mult, ALU.min)\
                    .then_inc(s2_step, 1)
                dve.reduce_sum(colmean[:, :], colsum[:, :], AX.X).then_inc(mean_step, 1)
                dve.wait_ge(mean_step, 1)
                dve.tensor_scalar(colmean_rep[:, :], ones[:, :], colmean[:, :], 1.0 / N,
                                  ALU.mult, ALU.mult).then_inc(mean_step, 1)

            def edge_bytes(n, q, first=False):
                c = CH * n + q
                slot = q % 2
                dve.wait_ge(adj_landed[q], 64 * n + 64)
                if not first:
                    dve.wait_ge(code_ready, c - 1)
                dve.tensor_scalar(noedge[:, slot, 0:S_DVE * CC],
                                  raw_slot[q][:, 0:S_DVE, :].rearrange("p s c -> p (s c)"),
                                  0.0, float(NOEDGE), ALU.is_le, ALU.mult).then_inc(noedge_dve, 1)

            def codes(n, q):
                c = CH * n + q
                slot = q % 2
                dve.wait_ge(noedge_dve, c + 1)
                dve.wait_ge(noedge_act, c + 1)
                dve.wait_ge(signs_ready, NS * c + NS)
                dve.scalar_tensor_tensor(code_words[slot], code_words[slot], MINUS4, noedge_words[slot],
                                         ALU.bitwise_xor, ALU.bitwise_or).then_inc(code_ready, 1)

            def masks(n, q, first=False):
                c = CH * n + q
                slot = q % 2
                dve.wait_ge(code_ready, c + 1)
                if not first:
                    dve.wait_ge(chunk_summed, c - 1)
                dve.transpose(minus[:, slot, :].rearrange("p (t s a) -> p s t a", s=NS, a=32),
                              code_words[slot].rearrange("p (s t b) -> p s t b", s=NS, b=32))\
                    .then_inc(code_turned, 1)
                dve.wait_ge(code_turned, c + 1)
                dve.tensor_scalar(plus[:, slot, :], minus[:, slot, :], PLUS4, PLUS4,
                                  ALU.bitwise_and, ALU.bitwise_xor).then_inc(masks_ready, 1)
                dve.tensor_scalar(minus[:, slot, :], minus[:, slot, :], MINUS4, MINUS4,
                                  ALU.bitwise_and, ALU.bitwise_xor).then_inc(masks_ready, 1)

            def chunk(n, q):
                edge_bytes(n, q)
                codes(n, q)
                masks(n, q)

            def add_minus(b, par):
                dve.wait_ge(plus_scaled, b + 1)
                dve.scalar_tensor_tensor(both[:, par, :], acc_minus[par][:, 0:2 * R], a_minus[:, bass.ds(b, 1)],
                                         scaled_plus[:, par, :], ALU.mult, ALU.add).then_inc(both_added, 1)
                dve.wait_ge(both_added, b + 1)
                dve.tensor_tensor(sums[:, par, :], both[:, par, 0:R], both[:, par, R:2 * R],
                                  ALU.add).then_inc(sums_ready, 1)

            def finish(pair):
                base = FINISH_STEPS * pair
                dve.wait_ge(sums_ready, 2 * pair + 2)
                dve.tensor_scalar(empty[:, :], sums[:, :, F], 0.0, None, ALU.is_equal).then_inc(finish_step, 1)
                dve.scalar_tensor_tensor(den[:, :], sums[:, :, F], 0.0, sums[:, :, F],
                                         ALU.is_equal, ALU.add).then_inc(finish_step, 1)
                dve.wait_ge(finish_step, base + 2)
                dve.reciprocal(rden[:, :], den[:, :]).then_inc(finish_step, 1)
                dve.wait_ge(finish_step, base + 3)
                dve.tensor_scalar(rscale[:, :], rden[:, :], h_bound[:, :], None, ALU.mult).then_inc(finish_step, 1)
                dve.wait_ge(finish_step, base + 4)
                for par in range(2):
                    dve.tensor_scalar(fallback[:, par, :], mean_h[:, :], empty[:, par:par + 1], None,
                                      ALU.mult).then_inc(finish_step, 1)
                dve.wait_ge(finish_step, base + 6)
                for par in range(2):
                    ins = dve.scalar_tensor_tensor(y[:, par, :], sums[:, par, 0:F], rscale[:, par:par + 1],
                                                   fallback[:, par, :], ALU.mult, ALU.add)
                ins.then_inc(finish_step, 1)
                dve.wait_ge(finish_step, base + 7)
                dve.tensor_scalar(ymin[:, :, :], y[:, :, :], 0.0, None, ALU.min).then_inc(finish_step, 1)

            def finish_elu(pair):
                base = FINISH_STEPS * pair
                dve.wait_ge(elu_exp, pair + 1)
                dve.tensor_scalar(yexp[:, :, :], yexp[:, :, :], -1.0, None, ALU.add).then_inc(finish_step, 1)
                dve.wait_ge(finish_step, base + 9)
                dve.scalar_tensor_tensor(elu1[:, :, :], y[:, :, :], 0.0, yexp[:, :, :],
                                         ALU.max, ALU.add).then_inc(finish_step, 1)
                dve.wait_ge(finish_step, base + 10)
                dve.wait_ge(xres_landed, 16 * pair + 16)

            def put_result(pair, first=False):
                if not first:
                    dve.wait_ge(result_stored, 16 * pair)
                dve.tensor_tensor(result[:, :, :], elu1[:, :, :], xres[:, :, :], ALU.add)\
                    .then_inc(result_ready, 1)

            variances(0)
            weights()
            inverse_roots(0)
            variances(1)
            s1_of(0)
            evacuate((0,))
            bound()
            inverse_roots(1)
            s1_of(2)
            evacuate((2,))
            variances(2)
            s1_of(4)
            evacuate((4,))
            inverse_roots(2)
            s1_of(6)
            evacuate((6,))
            variances(3)
            s1_of(8)
            evacuate((8,))
            inverse_roots(3)
            s1_of(10)
            evacuate((10,))
            s1_of(12)
            evacuate((12,))
            s1_of(14)
            evacuate((14,))
            dve.wait_ge(s1_step, 3 * G // 2)
            odd = s1col[:, :].rearrange("p (g m o) -> p m g o", g=NQ, o=2)[:, :, :, 1]
            dve.reduce_sum(odd, s1_folded, AX.X).then_inc(s1_summed, 1)

            for i in range(4):
                dve.wait_ge(s2_copied, i + 1)
                part = s2row[:, 512 * i:512 * (i + 1)]
                dve.reduce_max(small[:, 8 + i:9 + i], part, AX.X).then_inc(s2_part, 1)
                dve.transpose(s2_turned[:, 16 * i:16 * (i + 1), :].rearrange("p (t k) a -> p t k a", k=NK),
                              part.rearrange("p (t b k) -> p t k b", b=32, k=NK)).then_inc(s2_part, 1)
            dve.wait_ge(s2_part, 8)
            dve.reduce_max(small[:, 0:1], small[:, 8:12], AX.X).then_inc(s2_step, 1)
            dve.wait_ge(s1b_mm, 1)
            dve.tensor_copy(s1bias[:, :, :].rearrange("p b s -> p s b"),
                            s1b_ps.rearrange("p (s b) -> p s b", s=NS)).then_inc(s1bias_ready, 1)
            dve.wait_ge(s2max_ready, 1)
            dve.tensor_scalar(small[:, 4:5], small[:, 1:2], -1.0, None, ALU.mult).then_inc(s2_step, 1)
            dve.tensor_scalar(small[:, 5:6], small[:, 1:2], -ALPHA, None, ALU.mult).then_inc(s2_step, 1)
            dve.wait_ge(s1_summed, 1)
            dve.tensor_scalar(zmax[:, 0, :], s1col[:, :], small[:, 1:2], None, ALU.add).then_inc(s2_step, 1)

            edge_bytes(0, 0, first=True)

            dve.wait_ge(bexp_ready, 2)
            dve.wait_ge(weights_step, 8)
            for w in range(2):
                dve.tensor_scalar(bscaled[:, w, :], bexp[:, w, :], small[:, 6:7], FP16_TOP,
                                  ALU.mult, ALU.mult).then_inc(bscaled_ready, 1)
            dve.wait_ge(bscaled_ready, 2)

            def scaled_factors(gr):
                dve.wait_ge(h_mm, gr + 1)
                if gr >= 2:
                    dve.wait_ge(low_pool, lows_pool(gr - 2))
                    if gr % 2 == 0:
                        dve.wait_ge(low_dve, lows_dve(gr - 2))
                h4 = work[gr % 4][:, :].rearrange("p (k f) -> p k f", k=NK)
                for w in range(2):
                    factor = bscaled[:, w, NK * gr:NK * gr + NK].rearrange("p (k o) -> p k o", o=1)\
                        .to_broadcast([P, NK, F])
                    dve.tensor_tensor(uv32[:, gr % 2, w, :, :], h4, factor, ALU.mult).then_inc(uv32_ready, 1)

            def low(gr):
                dve.wait_ge(high_ready, 2 * gr + 2)
                low_part(dve, gr, 1).then_inc(low_dve, 1)

            scaled_factors(0)
            denominators(0)
            constants()
            low(0)
            scaled_factors(1)
            codes(0, 0)
            masks(0, 0, first=True)
            scaled_factors(2)
            edge_bytes(0, 1, first=True)
            low(2)
            scaled_factors(3)
            codes(0, 1)
            masks(0, 1, first=True)
            dve.wait_ge(mean_mm, 1)
            dve.tensor_copy(mean_h[:, :], mean_ps).then_inc(mean_step, 1)
            scaled_factors(4)
            scaled_factors(5)
            low(4)
            scaled_factors(6)
            edge_bytes(0, 2)
            low(6)
            scaled_factors(7)
            dve.wait_ge(h_mm, G // 2)
            denominators(1)
            codes(0, 2)
            scaled_factors(8)
            low(8)
            masks(0, 2)
            scaled_factors(9)
            edge_bytes(0, 3)
            scaled_factors(10)
            codes(0, 3)
            masks(0, 3)
            low(10)
            scaled_factors(11)
            scaled_factors(12)
            low(12)
            scaled_factors(13)
            edge_bytes(1, 0)
            scaled_factors(14)
            low(14)
            scaled_factors(15)
            codes(1, 0)
            dve.wait_ge(aexp_ready, 2)
            dve.tensor_scalar(a_minus[:, :], a_minus[:, :], MINUS_RESCALE, None, ALU.mult).then_inc(aexp_ready, 1)
            masks(1, 0)
            dve.wait_ge(aexp_ready, 3)
            add_minus(0, 0)
            add_minus(1, 1)

            def iteration(n, first=False):
                if not first:
                    chunk(n, 0)
                chunk(n, 1)
                if not first:
                    add_minus(2 * n - 1, 1)
                finish(n - 1)
                chunk(n, 2)
                chunk(n, 3)
                finish_elu(n - 1)
                put_result(n - 1, first=first)
                add_minus(2 * n, 0)

            iteration(1, first=True)
            with dve.Fori(2, NI) as n:
                iteration(n)
            add_minus(NB - 1, 1)
            finish(NI - 1)
            finish_elu(NI - 1)
            put_result(NI - 1)

        @block.tensor
        def _(pe):
            pe.wait_ge(w_landed, 48)
            pe.wait_ge(ident_ready, 2)
            pe.transpose(misc_ps[:, 0:F], w_sb[:, :], ident[:, :]).then_inc(pe_weights, 1)
            pe.wait_ge(weights_step, 3)
            pe.matmul(misc_ps[:, 256:256 + F], ones[:, :], w_sq[:, :], start=True, stop=True)\
                .then_inc(pe_weights, 1)
            pe.matmul(misc_ps[:, 128:129], w_t[:, :], a_sb[:, 1:2], start=True, stop=True).then_inc(pe_weights, 1)
            pe.matmul(misc_ps[:, 384:384 + F], a1_rep[:, :], w_t[:, :], start=True, stop=True)\
                .then_inc(pe_weights, 1)

            def evacuated(upto):
                if upto >= 1:
                    pe.wait_ge(evac_dve, (upto + 1) // 2)
                if upto >= 2:
                    pe.wait_ge(evac_act, upto // 2)

            def s2_along(i):
                evacuated(4 * i + 4)
                if i >= 2:
                    pe.wait_ge(s2_copied, i - 1)
                part = hn_t_low if i < 2 else hn_t_high[:, :, :]
                view = part.rearrange("f m (k g b) -> f g (m k) b", k=NK, g=NQ)
                first = 4 * NK * (i % 2)
                for g in range(NQ):
                    ins = pe.matmul(s2_ps[i % 2][32 * g:32 * g + 32, :], wa2_rep[:, :],
                                    view[:, g, first:first + 4 * NK, :], start=True, stop=True)
                ins.then_inc(s2_mm, 1)

            def h_group(gr):
                if gr >= 4:
                    pe.wait_ge(uv32_ready, 2 * gr - 6)
                for k in range(NK):
                    ins = pe.matmul(work[gr % 4][:, P * k:P * (k + 1)], hn_t[gr][:, P * k:P * (k + 1)],
                                    w_sb[:, :], start=True, stop=True)
                ins.then_inc(h_mm, 1)

            for gr in range(G):
                pe.wait_ge(hn_ready, gr + 1)
                evacuated(gr - 3)
                for k in range(NQ):
                    ins = pe.transpose(work[gr % 4][:, P * k:P * (k + 1)], hn[:, gr % 4, k, :], ident[:, :])
                ins.then_inc(turned, 1)
                if gr == 2:
                    pe.wait_ge(weights_step, 4)
                if gr % GP == 2 and gr >= GP:
                    s2_along(gr // GP - 1)
            s2_along(3)
            pe.wait_ge(s1_summed, 1)
            pe.wait_ge(s1_product_done, NQ * G // 2)
            pe.wait_ge(ident_ready, 2 + NS * NQ)
            for s in range(NS):
                ins = pe.matmul(s1b_ps[:, NB * s:NB * (s + 1)], sel[:, s, :, :].rearrange("p g b -> p (g b)"),
                                s1col[:, :], start=True, stop=True)
            ins.then_inc(s1b_mm, 1)
            for gr in range(4):
                h_group(gr)
            pe.wait_ge(mean_step, 2)
            pe.matmul(mean_ps, colmean_rep[:, :], w_sb[:, :], start=True, stop=True).then_inc(mean_mm, 1)

            plus8 = [plus[:, i, :].bitcast(dt.float8e4).rearrange("p (t i k) -> p t k i", t=NT, k=NK)
                     for i in range(2)]
            minus8 = [minus[:, i, :].bitcast(dt.float8e4).rearrange("p (t i k) -> p t k i", t=NT, k=NK)
                      for i in range(2)]

            def products(par, slot, gr):
                for k in range(NK):
                    j = NK * gr + k
                    ends = dict(start=(j == 0), stop=(j == NJ - 1))
                    pe.matmul(acc_plus[par][:, 0:2 * R], plus8[slot][:, gr % NT, k, :], uv[:, j, 0:2 * R], **ends)
                    ins = pe.matmul(acc_minus[par][:, 0:2 * R], minus8[slot][:, gr % NT, k, :],
                                    uv[:, j, 2 * R:4 * R], **ends)
                return ins

            def chunk(n, q):
                pe.wait_ge(masks_ready, 2 * CH * n + 2 * q + 2)
                pe.ldweights(uv[:, 0, 0:P], tile_position=(0, 0))
                for t in range(NT):
                    ins = products(q // NH, q % 2, NT * (q % NH) + t)
                ins.then_inc(chunk_summed, 1)

            pe.wait_ge(s2_copied, 4)
            pe.wait_ge(s1bias_ready, 2)
            pe.wait_ge(mean_step, 3)
            for gr in range(G):
                pe.wait_ge(low_pool, lows_pool(gr))
                pe.wait_ge(low_dve, lows_dve(gr))
                if gr % NT == 0:
                    pe.wait_ge(den_ready, 4 * (gr // NT) + 4)
                for par in range(2):
                    if gr % NT == 0:
                        pe.wait_ge(masks_ready, 4 * (gr // NT) + 2 * par + 2)
                    ins = products(par, par, gr)
                    if gr % NT == NT - 1:
                        ins.then_inc(chunk_summed, 1)
                if gr + 4 < G:
                    h_group(gr + 4)
            with pe.Fori(1, NI) as n:
                for q in range(CH):
                    if q % NH == 0:
                        pe.wait_ge(both_added, 2 * n + q // NH - 1)
                    chunk(n, q)


_INS = ['x', 'adj', 'L0_gnn_W', 'L0_gnn_a']


def kernel(**inputs):
    import numpy as _np
    import concourse.bacc as _bacc
    from concourse.bass_utils import run_bass_kernel_spmd as _run

    nc = _bacc.Bacc("TRN2", target_bir_lowering=False, num_devices=1)
    arrays, args = {}, []
    for name in _INS:
        arr = _np.ascontiguousarray(inputs[name])
        arrays[f"in_{name}_dram"] = arr
        args.append(nc.dram_tensor(f"in_{name}_dram", arr.shape, mybir.dt.from_np(arr.dtype),
                                   kind="ExternalInput").ap())
    args.append(nc.dram_tensor("out_dram", tuple(inputs['x'].shape), dt.float32, kind="ExternalOutput").ap())
    build(nc, *args)
    r = _run(nc, [arrays], core_ids=[0])
    return r.results[0]["out_dram"]
```

```python
import concourse.bass as bass
from concourse import mybir
from contextlib import ExitStack

dt = mybir.dt
ALU = mybir.AluOpType
ACT = mybir.ActivationFunctionType
AX = mybir.AxisListType
RMAX = bass.bass_isa.ReduceOp.max

ALPHA = 0.2
EPS = 1e-5

PLUS, MINUS = 0x20, 0x10
NOEDGE = PLUS | MINUS
PLUS4, MINUS4 = PLUS * 0x01010101, MINUS * 0x01010101
MINUS_RESCALE = 4.0
FP16_TOP = 32768.0


def build(nc, x, adj, W, a, out):
    N, F = x.shape
    P = 128
    NB = N // P
    NQ = 4
    QC = N // NQ
    NH = 2
    CC = QC // NH
    NS = 4
    NT = CC // 128
    NK = 4
    NJ = NH * NT * NK
    NI = NB // 2
    CH = 2 * NH
    R = F + 1
    CW = CC // 4
    G = NJ // NK
    XP = 4
    GP = G // XP
    f32, f16, u32 = dt.float32, dt.float16, dt.uint32

    x_tiles = x.rearrange("(b p) f -> p b f", p=P)
    x_quarters = x.rearrange("(g m p) f -> g p m f", g=NQ, p=P)
    out_tiles = out.rearrange("(b p) f -> p b f", p=P)
    adj_view = adj.rearrange("(b s a) (g h c) -> g h a b s c", s=NS, a=32, g=NQ, h=NH)

    ctx = ExitStack()
    with ctx:
        def sb(name, shape, d):
            return ctx.enter_context(nc.sbuf_tensor(name, shape, d))

        def bank(name):
            return ctx.enter_context(nc.psum_tensor(name, [P, 512], f32))

        def sem(name):
            return ctx.enter_context(nc.semaphore(name))

        raw = sb("raw", [P, CH * NS * CC], dt.int32)
        noedge = sb("noedge", [P, NH, NS * CC], dt.uint8)
        code = sb("code", [P, NH, NS * CC], dt.int8)
        minus = sb("minus", [P, NH, NS * CW], u32)
        plus = sb("plus", [P, NH, NS * CW], u32)
        uv = sb("uv", [P, NJ, 4 * R], f16)
        s2row = sb("s2row", [P, QC], f32)
        s1bias = sb("s1bias", [P, NB, NS], f32)
        a_plus = sb("a_plus", [P, NB], f32)
        a_now = sb("a_now", [P, 2], f32)
        a_minus = sb("a_minus", [P, NB], f32)
        h_bound = sb("h_bound", [P, 1], f32)
        mean_h = sb("mean_h", [P, F], f32)
        scaled_plus = sb("scaled_plus", [P, 2, 2 * R], f32)
        both = sb("both", [P, 2, 2 * R], f32)
        sums = sb("sums", [P, 2, R], f32)
        empty = sb("empty", [P, 2], f32)
        den = sb("den", [P, 2], f32)
        rden = sb("rden", [P, 2], f32)
        rscale = sb("rscale", [P, 2], f32)
        ident = sb("ident", [P, P], f32)
        ones = sb("ones", [P, P], f32)
        w_sb = sb("w_sb", [P, F], f32)
        a_sb = sb("a_sb", [P, 2], f32)
        wa_rep = sb("wa_rep", [P, 2, 32], f32)
        colsum = sb("colsum", [P, G], f32)
        colmean = sb("colmean", [P, 1], f32)
        s1col = sb("s1col", [P, NB], f32)
        small = sb("small", [P, 13], f32)
        hn_t_high = sb("hn_t_high", [P, G // 2, NK * P], f32)
        bexp = sb("bexp", [P, 2, NJ], f32)
        bscaled = sb("bscaled", [P, 2, NJ], f32)
        uv_more = sb("uv_more", [P, 2, NK, F], f32)
        zmax = sb("zmax", [P, 3, NB], f32)
        hn = sb("hn", [P, 4, NQ, F], f32)

        slot_words = NS * CC
        raw_slot = [raw[:, q * slot_words:(q + 1) * slot_words].rearrange("p (s c) -> p s c", s=NS)
                    for q in range(CH)]
        uv_flat = uv[:, :, :].rearrange("p j c -> p (j c)")
        x_sb = uv_flat[:, 0:2 * NB * F].bitcast(f32).rearrange("p (m g f) -> p m g f", g=NQ, f=F)
        low_start = 3 * NJ // 4 * 4 * R
        hn_t_low = uv_flat[:, low_start:low_start + N].bitcast(f32).rearrange("p (m n) -> p m n", n=NK * P)
        hn_t = [hn_t_low[:, m, :] for m in range(G // 2)] + [hn_t_high[:, m, :] for m in range(G // 2)]
        ring2 = [t[:, :, :].rearrange("p i c -> p (i c)")[:, 0:NK * F].rearrange("p (k f) -> p k f", f=F)
                 for t in (scaled_plus, both)]
        uv32 = [[hn[:, 0, :, :], hn[:, 1, :, :]], [hn[:, 2, :, :], hn[:, 3, :, :]], ring2,
                [uv_more[:, w, :, :] for w in range(2)]]
        UVR = len(uv32)
        fallback, y, ymin, yexp, positive, xres, result = [
            hn[:, i // 2, 2 * (i % 2):2 * (i % 2) + 2, :] for i in range(7)]
        early = uv_flat[:, low_start - N:low_start].bitcast(f32)
        sel = early[:, 0:NQ * P].rearrange("p (g q a) -> p g q a", g=NQ, q=NQ)
        ln = early[:, NQ * P:NQ * P + 8 * NB].rearrange("p (i b) -> p i b", b=NB)
        stats = early[:, NQ * P + 8 * NB:NQ * P + 14 * NB].rearrange("p (b i) -> p b i", i=6)
        s1_turned = early[:, NQ * P + 14 * NB:NQ * P + 22 * NB].rearrange("p (t a) -> p t a", a=32)
        later = NQ * P + 22 * NB
        w_t, w_sq, colmean_rep = [early[:, later + P * i:later + P * (i + 1)] for i in range(3)]
        s2_turned = uv_flat[:, 0:2 * NJ * 32].bitcast(f32).rearrange("p (j a) -> p j a", a=32)
        noedge_words = [noedge[:, h, :].bitcast(u32) for h in range(NH)]
        code_words = [code[:, h, :].bitcast(u32) for h in range(NH)]

        acc_plus = [bank(f"acc_plus{i}") for i in range(2)]
        acc_minus = [bank(f"acc_minus{i}") for i in range(2)]
        work = [bank(f"work{i}") for i in range(4)]
        s2_ps = [acc_plus[0], acc_minus[0]]
        s1_ps = acc_plus[1]
        misc_ps = acc_minus[1]
        mean_ps = acc_minus[1][:, 0:F]
        s1b_ps = acc_minus[1][:, 512 - NS * NB:512]

        x_started = [sem(f"x_started{g}") for g in range(NQ)]
        x_landed = {i: sem(f"x_landed{i}") for i in range(1, XP)}
        w_landed = sem("w_landed")
        adj_landed = [sem(f"adj_landed{q}") for q in range(CH)]
        ident_ready = sem("ident_ready")
        ones_ready = sem("ones_ready")
        weights_step = sem("weights_step")
        pe_weights = sem("pe_weights")
        bound_root = sem("bound_root")
        stats_step = sem("stats_step")
        var_ready = sem("var_ready")
        root_ready = sem("root_ready")
        hn_act = sem("hn_act")
        scaled = sem("scaled")
        hn_pool = sem("hn_pool")
        turned = sem("turned")
        evac_dve = sem("evac_dve")
        evac_act = sem("evac_act")
        s1_mm = sem("s1_mm")
        s1_transposed = sem("s1_transposed")
        s1_spread_mm = sem("s1_spread_mm")
        s1bias_ready = sem("s1bias_ready")
        s2_mm = sem("s2_mm")
        s2_copied = sem("s2_copied")
        s1col_ready = sem("s1col_ready")
        minus_one = sem("minus_one")
        s2_step = sem("s2_step")
        s2max_ready = sem("s2max_ready")
        bexp_ready = sem("bexp_ready")
        aexp_ready = sem("aexp_ready")
        mean_step = sem("mean_step")
        mean_mm = sem("mean_mm")
        rstd_ready = sem("rstd_ready")
        s2_maxima = sem("s2_maxima")
        s2_turned_parts = sem("s2_turned_parts")
        bscaled_ready = sem("bscaled_ready")
        den_ready = sem("den_ready")
        h_mm = sem("h_mm")
        uv32_ready = sem("uv32_ready")
        high_ready = sem("high_ready")
        low_pool = sem("low_pool")
        low_dve = sem("low_dve")
        noedge_dve = sem("noedge_dve")
        noedge_act = sem("noedge_act")
        signs_ready = sem("signs_ready")
        code_ready = sem("code_ready")
        code_turned = sem("code_turned")
        masks_ready = sem("masks_ready")
        chunk_summed = sem("chunk_summed")
        pair_factors = sem("pair_factors")
        plus_scaled = sem("plus_scaled")
        both_added = sem("both_added")
        sums_ready = sem("sums_ready")
        finish_step = sem("finish_step")
        elu_exp = sem("elu_exp")
        xres_landed = sem("xres_landed")
        result_ready = sem("result_ready")
        result_stored = sem("result_stored")

        FINISH_STEPS = 9
        POOL_GROUPS = (2, 3, 6, 7, 10, 11, 14, 15)
        DVE_EVACS = (11, 13, 15)
        LOW_DVE = (0, 2, 4, 14)
        S_ACT = 1
        S_DVE = NS - S_ACT

        block = ctx.enter_context(nc.Block())


        def parity(n, q):
            return q % 2 if isinstance(n, int) and n == 0 else q // NH

        def half(n, q):
            return q // 2 if isinstance(n, int) and n == 0 else q % NH

        def load_adj(eng, n, q, quarters):
            for g in quarters:
                eng.dma_start(raw_slot[q][32 * g:32 * g + 32, :, :],
                              adj_view[g, half(n, q), :, 2 * n + parity(n, q), :, :]).then_inc(adj_landed[q], 16)

        def load_x(eng, i, quarters, landed):
            for g in quarters:
                eng.dma_start(x_sb[:, GP * i:GP * (i + 1), g, :], x_quarters[g, :, GP * i:GP * (i + 1), :])\
                    .then_inc(landed, 16)

        def by_set(group):
            return group.rearrange("f (k g b) -> f k g b", k=NK, g=NQ)

        def by_node(bank_):
            return bank_[:, :].rearrange("f (g b k) -> f k g b", g=NQ, k=NK)

        def by_quarter(row, i):
            return row.rearrange("p (g t) -> p g t", g=NQ)[:, :, NK * XP * i:NK * XP * (i + 1)]

        def pool_groups(gr):
            return len([g for g in POOL_GROUPS if g <= gr])

        def wait_normalised(eng, gr):
            eng.wait_ge(hn_act, gr + 1 - pool_groups(gr))
            if pool_groups(gr):
                eng.wait_ge(hn_pool, pool_groups(gr))

        def evacs_dve(gr):
            return len([g for g in DVE_EVACS if g <= gr])

        def wait_evacuated(eng, gr):
            if evacs_dve(gr):
                eng.wait_ge(evac_dve, evacs_dve(gr))
            if gr + 1 > evacs_dve(gr):
                eng.wait_ge(evac_act, gr + 1 - evacs_dve(gr))

        def lows_dve(gr):
            return len([g for g in LOW_DVE if g <= gr])

        def lows_pool(gr):
            return 2 * (gr + 1) - lows_dve(gr)

        def low_part(eng, gr, w):
            lo = uv[:, NK * gr:NK * gr + NK, 2 * R * w + R:2 * R * w + R + F]
            hi = uv[:, NK * gr:NK * gr + NK, 2 * R * w:2 * R * w + F]
            return eng.tensor_tensor(lo, uv32[gr % UVR][w], hi, ALU.subtract)

        @block.sync
        def _(sp):
            for g in range(NQ):
                load_x(sp, 0, (g,), x_started[g])
            sp.dma_start(w_sb[:, :], W).then_inc(w_landed, 16)
            for i in range(2):
                sp.dma_start(a_sb[:, i:i + 1], a[i * F:(i + 1) * F, :]).then_inc(w_landed, 16)
            for i in range(1, XP):
                load_x(sp, i, range(NQ), x_landed[i])
            for q in range(CH):
                load_adj(sp, 0, q, range(NQ))

            def load_iteration(n):
                for q in range(CH):
                    sp.wait_ge(noedge_dve, CH * n + q - CH + 1)
                    sp.wait_ge(noedge_act, CH * n + q - CH + 1)
                    load_adj(sp, n, q, (0, 1))

            load_iteration(1)
            sp.wait_ge(low_pool, lows_pool(G - 1))
            sp.wait_ge(low_dve, lows_dve(G - 1))
            sp.dma_start(xres[:, :, :], x_tiles[:, 0:2, :]).then_inc(xres_landed, 16)
            with sp.Fori(2, NI) as n:
                load_iteration(n)
                sp.wait_ge(result_ready, n - 1)
                sp.dma_start(out_tiles[:, bass.ds(2 * n - 4, 2), :], result[:, :, :])\
                    .then_inc(result_stored, 16)
                sp.dma_start(xres[:, :, :], x_tiles[:, bass.ds(2 * n - 2, 2), :]).then_inc(xres_landed, 16)
            sp.wait_ge(result_ready, NI - 1)
            sp.dma_start(out_tiles[:, NB - 4:NB - 2, :], result[:, :, :]).then_inc(result_stored, 16)
            sp.dma_start(xres[:, :, :], x_tiles[:, NB - 2:NB, :]).then_inc(xres_landed, 16)
            sp.wait_ge(result_ready, NI)
            sp.dma_start(out_tiles[:, NB - 2:NB, :], result[:, :, :]).then_inc(result_stored, 16)
            sp.wait_ge(result_stored, 16 * NI)

        @block.gpsimd
        def _(pool):
            pool.memset(ident[:, :], 0.0).then_inc(ident_ready, 1)
            pool.wait_ge(ident_ready, 1)
            pool.affine_select(out=ident[:, :], in_=ident[:, :], compare_op=ALU.not_equal, fill=1.0,
                               base=0, pattern=[[-1, P]], channel_multiplier=1).then_inc(ident_ready, 1)
            pool.wait_ge(ident_ready, 2)
            for g in range(NQ):
                for q in range(NQ):
                    pool.tensor_copy(sel[:, g, q, :], ident[:, 32 * g:32 * g + 32]).then_inc(ident_ready, 1)

            for i, gr in enumerate(POOL_GROUPS):
                def along(row):
                    return ln[:, row, NQ * gr:NQ * gr + NQ].rearrange("p (g o) -> p g o", o=1)\
                        .to_broadcast([P, NQ, F])

                pool.wait_ge(rstd_ready, gr // GP + 1)
                if gr >= 4:
                    pool.wait_ge(turned, gr - 3)
                pool.tensor_tensor(hn[:, gr % 4, :, :], x_sb[:, gr, :, :], along(7), ALU.mult)\
                    .then_inc(scaled, 1)
                pool.wait_ge(scaled, i + 1)
                pool.tensor_tensor(hn[:, gr % 4, :, :], hn[:, gr % 4, :, :], along(3), ALU.add)\
                    .then_inc(hn_pool, 1)
            pool.wait_ge(s2_step, 1)
            pool.partition_all_reduce(small[:, 1:2], small[:, 0:1], P, RMAX).then_inc(s2max_ready, 1)
            for gr in range(G):
                for w in range(1 if gr in LOW_DVE else 2):
                    pool.wait_ge(high_ready, 2 * gr + w + 1)
                    low_part(pool, gr, w).then_inc(low_pool, 1)

        @block.scalar
        def _(act):
            def edge_bytes(n, q, load=None, first=False):
                c = CH * n + q
                slot = q % 2
                if load is not None:
                    act.wait_ge(noedge_dve, c - 1)
                    act.wait_ge(noedge_act, c - 1)
                    load_adj(act, *load, (2, 3))
                act.wait_ge(adj_landed[q], 64 * n + 64)
                if not first:
                    act.wait_ge(code_turned, c - 1)
                act.activation(noedge[:, slot, S_DVE * CC:].bitcast(dt.int8),
                               raw_slot[q][:, S_DVE:, :].rearrange("p s c -> p (s c)"),
                               ACT.Sign, scale=2.0, bias=small[:, 7:8]).then_inc(noedge_act, 1)

            def signs(n, q, groups):
                h, slot = half(n, q), q % 2
                for s in groups:
                    act.activation(code[:, slot, s * CC:(s + 1) * CC], s2row[:, h * CC:(h + 1) * CC],
                                   ACT.Sign, bias=s1bias_at(n, q, s)).then_inc(signs_ready, 1)

            def chunk(n, q, load=None):
                edge_bytes(n, q, load)
                signs(n, q, range(NS))

            def s1bias_at(n, q, s):
                b = 2 * n + parity(n, q)
                return s1bias[:, bass.ds(b, 1), s:s + 1].rearrange("p b s -> p (b s)")

            def scale_plus(pair, par):
                first = isinstance(pair, int) and pair == 0
                act.wait_ge(chunk_summed, CH * pair + (3 + par if first else NH * par + NH))
                act.wait_ge(pair_factors, pair + 1)
                act.activation(scaled_plus[:, par, :], acc_plus[par][:, 0:2 * R], ACT.Copy,
                               scale=a_now[:, par:par + 1]).then_inc(plus_scaled, 1)

            def fetch_factors(pair):
                act.activation(a_now[:, :], a_plus[:, bass.ds(2 * pair, 2)], ACT.Copy)\
                    .then_inc(pair_factors, 1)

            def elu_exponential(pair):
                act.wait_ge(finish_step, FINISH_STEPS * pair + 8)
                act.activation(yexp[:, :, :], ymin[:, :, :], ACT.Exp).then_inc(elu_exp, 1)

            def root(i):
                part = slice(i * NB // XP, (i + 1) * NB // XP)
                act.wait_ge(var_ready, i + 1)
                act.activation(ln[:, 2, part], ln[:, 1, part], ACT.Sqrt).then_inc(root_ready, 1)

            def normalise(gr):
                act.wait_ge(rstd_ready, gr // GP + 1)
                if gr >= 4:
                    act.wait_ge(turned, gr - 3)
                for g in range(NQ):
                    b = NQ * gr + g
                    ins = act.activation(hn[:, gr % 4, g, :], x_sb[:, gr, g, :], ACT.Identity,
                                         scale=ln[:, 7, b:b + 1], bias=ln[:, 3, b:b + 1])
                ins.then_inc(hn_act, 1)

            def evacuate(gr):
                act.wait_ge(turned, gr + 1)
                act.activation(by_set(hn_t[gr]), by_node(work[gr % 4]), ACT.Relu,
                               accum_out=colsum[:, gr:gr + 1]).then_inc(evac_act, 1)

            def s2_rows(i):
                act.wait_ge(s2_mm, i + 1)
                act.activation(s2row[:, 512 * i:512 * (i + 1)].rearrange("p (m b k) -> p m k b", k=NK, b=32),
                               s2_ps[i % 2][:, :].rearrange("p (m k b) -> p m k b", k=NK, b=32),
                               ACT.Copy).then_inc(s2_copied, 1)

            root(0)
            for gr in range(G):
                if gr not in POOL_GROUPS:
                    normalise(gr)
                if gr % GP == 1 and gr // GP + 1 < XP:
                    root(gr // GP + 1)
                if gr == 4:
                    act.wait_ge(weights_step, 4)
                    act.activation(small[:, 3:4], small[:, 2:3], ACT.Sqrt, scale=float(F)).then_inc(bound_root, 1)
                if gr >= 2 and gr - 2 not in DVE_EVACS:
                    evacuate(gr - 2)
                if gr in (10, 14):
                    s2_rows(gr // 4 - 2)
            act.wait_ge(minus_one, 1)
            for gr in (G - 2, G - 1):
                if gr not in DVE_EVACS:
                    evacuate(gr)
            act.wait_ge(s1bias_ready, 1)
            act.wait_ge(s2_copied, 2)
            signs(0, 0, (0,))
            s2_rows(2)
            act.activation(small[:, 12:13], small[:, 7:8], ACT.Exp)
            s2_rows(3)
            edge_bytes(0, 0, first=True)
            signs(0, 0, (1,))

            def high_parts(gr):
                for w in range(2):
                    act.wait_ge(uv32_ready, 2 * gr + w + 1)
                    act.activation(uv[:, NK * gr:NK * gr + NK, 2 * R * w:2 * R * w + F],
                                   uv32[gr % UVR][w], ACT.Copy).then_inc(high_ready, 1)

            act.wait_ge(s2_turned_parts, XP)
            act.wait_ge(s2_step, 3)
            act.activation(bexp[:, 0, :], s2_turned[:, :, 0], ACT.Exp, bias=small[:, 4:5]).then_inc(bexp_ready, 1)
            act.activation(bexp[:, 1, :], s2_turned[:, :, 0], ACT.Exp, bias=small[:, 5:6],
                           scale=ALPHA).then_inc(bexp_ready, 1)
            signs(0, 0, (2, 3))
            high_parts(0)
            edge_bytes(0, 1, first=True)
            signs(0, 1, (0,))
            high_parts(1)
            signs(0, 1, (1,))
            high_parts(2)
            signs(0, 1, (2, 3))
            high_parts(3)
            high_parts(4)
            edge_bytes(0, 2, load=(1, 0))
            signs(0, 2, (0,))
            high_parts(5)
            signs(0, 2, (1, 2))
            high_parts(6)
            signs(0, 2, (3,))
            high_parts(7)
            edge_bytes(0, 3, load=(1, 1))
            high_parts(8)
            signs(0, 3, (0, 1))
            high_parts(9)
            signs(0, 3, (2,))
            high_parts(10)
            signs(0, 3, (3,))
            high_parts(11)
            edge_bytes(1, 0, load=(1, 2))
            signs(1, 0, (0,))
            high_parts(12)
            signs(1, 0, (1,))
            high_parts(13)
            signs(1, 0, (2,))
            high_parts(14)
            high_parts(15)
            signs(1, 0, (3,))
            act.wait_ge(s2_step, 6)
            act.activation(a_plus[:, :], zmax[:, 1, :], ACT.Exp).then_inc(aexp_ready, 1)
            act.activation(a_minus[:, :], zmax[:, 2, :], ACT.Exp).then_inc(aexp_ready, 1)
            act.wait_ge(aexp_ready, 1)
            fetch_factors(0)
            edge_bytes(1, 1, load=(1, 3))
            signs(1, 1, (0,))
            scale_plus(0, 0)
            signs(1, 1, (1, 2, 3))
            scale_plus(0, 1)
            chunk(1, 2, load=(2, 0))
            chunk(1, 3, load=(2, 1))
            elu_exponential(0)

            def iteration(n, last=False):
                chunk(n, 0, load=(n, 2))
                fetch_factors(n - 1)
                scale_plus(n - 1, 0)
                chunk(n, 1, load=(n, 3))
                chunk(n, 2, load=None if last else (n + 1, 0))
                scale_plus(n - 1, 1)
                chunk(n, 3, load=None if last else (n + 1, 1))
                elu_exponential(n - 1)

            with act.Fori(2, NI - 1) as n:
                iteration(n)
            iteration(NI - 1, last=True)
            act.wait_ge(plus_scaled, NB - 2)
            fetch_factors(NI - 1)
            scale_plus(NI - 1, 0)
            scale_plus(NI - 1, 1)
            elu_exponential(NI - 1)

        @block.vector
        def _(dve):
            dve.memset(ones[:, :], 1.0).then_inc(ones_ready, 1)
            dve.memset(small[:, 7:8], -1.0).then_inc(minus_one, 1)

            step = [0]

            def after(ins):
                step[0] += 1
                ins.then_inc(stats_step, 1)
                dve.wait_ge(stats_step, step[0])

            def variances(i):
                part = slice(i * NB // XP, (i + 1) * NB // XP)
                if i:
                    dve.wait_ge(x_landed[i], 16 * NQ)
                for g in range(NQ):
                    if i == 0:
                        dve.wait_ge(x_started[g], 16)
                    for m in range(GP * i, GP * (i + 1)):
                        ins = dve.bn_stats(stats[:, NQ * m + g, :], x_sb[:, m, g, :])
                after(ins)
                mean_e, m2_e = stats[:, part, 1], stats[:, part, 2]
                mean_o, m2_o = stats[:, part, 4], stats[:, part, 5]
                dve.tensor_tensor(ln[:, 4, part], mean_e, mean_o, ALU.subtract)
                dve.tensor_tensor(ln[:, 5, part], m2_e, m2_o, ALU.add)
                after(dve.tensor_tensor(ln[:, 0, part], mean_e, mean_o, ALU.add))
                dve.tensor_scalar(ln[:, 5, part], ln[:, 5, part], 1.0 / F, EPS, ALU.mult, ALU.add)
                after(dve.scalar_tensor_tensor(ln[:, 6, part], ln[:, 4, part], 0.25, ln[:, 4, part],
                                               ALU.mult, ALU.mult))
                dve.tensor_tensor(ln[:, 1, part], ln[:, 6, part], ln[:, 5, part], ALU.add).then_inc(var_ready, 1)

            def inverse_roots(i):
                part = slice(i * NB // XP, (i + 1) * NB // XP)
                dve.wait_ge(root_ready, i + 1)
                after(dve.reciprocal(ln[:, 3, part], ln[:, 2, part]))
                after(dve.tensor_tensor(ln[:, 4, part], ln[:, 3, part], ln[:, 3, part], ALU.mult))
                after(dve.scalar_tensor_tensor(ln[:, 5, part], ln[:, 4, part], -0.5, ln[:, 1, part],
                                               ALU.mult, ALU.mult))
                after(dve.scalar_tensor_tensor(ln[:, 7, part], ln[:, 5, part], 1.5, ln[:, 3, part],
                                               ALU.add, ALU.mult))
                dve.scalar_tensor_tensor(ln[:, 3, part], ln[:, 0, part], -0.5, ln[:, 7, part],
                                         ALU.mult, ALU.mult).then_inc(rstd_ready, 1)

            def evacuate(groups):
                for gr in groups:
                    dve.wait_ge(turned, gr + 1)
                    dve.tensor_scalar(by_set(hn_t[gr]), by_node(work[gr % 4]), 0.0, None, ALU.max, ALU.add,
                                      accum_out=colsum[:, gr:gr + 1]).then_inc(evac_dve, 1)

            def weights():
                dve.wait_ge(w_landed, 48)
                dve.tensor_tensor(w_sq, w_sb[:, :], w_sb[:, :], ALU.mult).then_inc(weights_step, 1)
                dve.wait_ge(pe_weights, 1)
                dve.tensor_copy(w_t, misc_ps[:, 0:F]).then_inc(weights_step, 1)

            def weights_end():
                dve.wait_ge(ones_ready, 1)
                dve.wait_ge(pe_weights, 3)
                for i in range(2):
                    ins = dve.tensor_scalar(wa_rep[:, i, :], ones[:, 0:32], misc_ps[:, 128 + i:129 + i], None,
                                            ALU.mult)
                ins.then_inc(weights_step, 1)
                dve.reduce_max(small[:, 2:3], misc_ps[:, 256:256 + F], AX.X).then_inc(weights_step, 1)

            def bound():
                dve.wait_ge(bound_root, 1)
                dve.tensor_scalar(h_bound[:, :], small[:, 3:4], 1e-30, None, ALU.max).then_inc(weights_step, 1)
                dve.wait_ge(weights_step, 5)
                dve.reciprocal(small[:, 6:7], h_bound[:, :]).then_inc(weights_step, 1)

            def s1_turn(i):
                dve.wait_ge(s1_mm, i + 1)
                if i:
                    dve.wait_ge(s1_spread_mm, i)
                dve.transpose(s1_turned[:, :, :], s1_ps[:, :].rearrange("p (t a) -> p t a", a=32))\
                    .then_inc(s1_transposed, 1)

            def s1_copy(i):
                dve.wait_ge(s1_spread_mm, i + 1)
                dve.tensor_copy(by_quarter(s1bias[:, :, :].rearrange("p b s -> p (b s)"), i),
                                by_quarter(s1b_ps, i)).then_inc(s1bias_ready, 1)

            def s2_largest(i):
                dve.wait_ge(s2_copied, i + 1)
                dve.reduce_max(small[:, 8 + i:9 + i], s2row[:, 512 * i:512 * (i + 1)], AX.X).then_inc(s2_maxima, 1)

            def s2_turn(i):
                if i == 0:
                    wait_normalised(dve, GP - 1)
                dve.transpose(s2_turned[:, 16 * i:16 * (i + 1), :].rearrange("p (t k) a -> p t k a", k=NK),
                              s2row[:, 512 * i:512 * (i + 1)].rearrange("p (t b k) -> p t k b", b=32, k=NK))\
                    .then_inc(s2_turned_parts, 1)

            def denominators(h):
                sets = slice(NJ // NH * h, NJ // NH * (h + 1))
                for w in range(2):
                    dve.tensor_scalar(uv[:, sets, 2 * R * w + F], bexp[:, w, sets], FP16_TOP, None,
                                      ALU.mult).then_inc(den_ready, 1)
                dve.wait_ge(den_ready, 4 * h + 2)
                for w in range(2):
                    dve.scalar_tensor_tensor(uv[:, sets, 2 * R * w + R + F], bexp[:, w, sets], FP16_TOP,
                                             uv[:, sets, 2 * R * w + F], ALU.mult, ALU.subtract)\
                        .then_inc(den_ready, 1)

            def constants():
                dve.wait_ge(s1bias_ready, XP)
                for s in range(NS):
                    rows = slice(32 * s, 32 * s + 32)
                    ins = dve.tensor_copy(s1col[rows, :], s1bias[rows, :, s])
                ins.then_inc(s1col_ready, 1)
                dve.wait_ge(s1col_ready, 1)
                dve.tensor_scalar(zmax[:, 0, :], s1col[:, :], small[:, 1:2], None, ALU.add).then_inc(s2_step, 1)
                dve.wait_ge(s2_step, 4)
                dve.tensor_scalar(zmax[:, 1, :], zmax[:, 0, :], 1.0 - ALPHA, 0.0, ALU.mult, ALU.min)\
                    .then_inc(s2_step, 1)
                dve.tensor_scalar(zmax[:, 2, :], zmax[:, 0, :], ALPHA - 1.0, 0.0, ALU.mult, ALU.min)\
                    .then_inc(s2_step, 1)

            def edge_bytes(n, q, first=False):
                c = CH * n + q
                slot = q % 2
                dve.wait_ge(adj_landed[q], 64 * n + 64)
                if not first:
                    dve.wait_ge(code_ready, c - 1)
                dve.tensor_scalar(noedge[:, slot, 0:S_DVE * CC],
                                  raw_slot[q][:, 0:S_DVE, :].rearrange("p s c -> p (s c)"),
                                  0.0, float(NOEDGE), ALU.is_le, ALU.mult).then_inc(noedge_dve, 1)

            def codes(n, q):
                c = CH * n + q
                slot = q % 2
                dve.wait_ge(noedge_dve, c + 1)
                dve.wait_ge(noedge_act, c + 1)
                dve.wait_ge(signs_ready, NS * c + NS)
                dve.scalar_tensor_tensor(code_words[slot], code_words[slot], MINUS4, noedge_words[slot],
                                         ALU.bitwise_xor, ALU.bitwise_or).then_inc(code_ready, 1)

            def masks(n, q, first=False):
                c = CH * n + q
                slot = q % 2
                dve.wait_ge(code_ready, c + 1)
                if not first:
                    dve.wait_ge(chunk_summed, c - 1)
                dve.transpose(minus[:, slot, :].rearrange("p (t s a) -> p s t a", s=NS, a=32),
                              code_words[slot].rearrange("p (s t b) -> p s t b", s=NS, b=32))\
                    .then_inc(code_turned, 1)
                dve.wait_ge(code_turned, c + 1)
                dve.tensor_scalar(plus[:, slot, :], minus[:, slot, :], PLUS4, PLUS4,
                                  ALU.bitwise_and, ALU.bitwise_xor).then_inc(masks_ready, 1)
                dve.tensor_scalar(minus[:, slot, :], minus[:, slot, :], MINUS4, MINUS4,
                                  ALU.bitwise_and, ALU.bitwise_xor).then_inc(masks_ready, 1)

            def chunk(n, q):
                edge_bytes(n, q)
                codes(n, q)
                masks(n, q)

            def add_minus(b, par):
                dve.wait_ge(plus_scaled, b + 1)
                dve.scalar_tensor_tensor(both[:, par, :], acc_minus[par][:, 0:2 * R], a_minus[:, bass.ds(b, 1)],
                                         scaled_plus[:, par, :], ALU.mult, ALU.add).then_inc(both_added, 1)
                dve.wait_ge(both_added, b + 1)
                dve.tensor_tensor(sums[:, par, :], both[:, par, 0:R], both[:, par, R:2 * R],
                                  ALU.add).then_inc(sums_ready, 1)

            def finish(pair, first=False):
                base = FINISH_STEPS * pair
                if not first:
                    dve.wait_ge(result_ready, pair)
                dve.wait_ge(sums_ready, 2 * pair + 2)
                dve.tensor_scalar(empty[:, :], sums[:, :, F], 0.0, None, ALU.is_equal).then_inc(finish_step, 1)
                dve.scalar_tensor_tensor(den[:, :], sums[:, :, F], 0.0, sums[:, :, F],
                                         ALU.is_equal, ALU.add).then_inc(finish_step, 1)
                dve.wait_ge(finish_step, base + 2)
                dve.reciprocal(rden[:, :], den[:, :]).then_inc(finish_step, 1)
                for par in range(2):
                    dve.tensor_scalar(fallback[:, par, :], mean_h[:, :], empty[:, par:par + 1], None,
                                      ALU.mult).then_inc(finish_step, 1)
                dve.wait_ge(finish_step, base + 3)
                dve.tensor_scalar(rscale[:, :], rden[:, :], h_bound[:, :], None, ALU.mult).then_inc(finish_step, 1)
                dve.wait_ge(finish_step, base + 6)
                for par in range(2):
                    ins = dve.scalar_tensor_tensor(y[:, par, :], sums[:, par, 0:F], rscale[:, par:par + 1],
                                                   fallback[:, par, :], ALU.mult, ALU.add)
                ins.then_inc(finish_step, 1)
                dve.wait_ge(finish_step, base + 7)
                dve.tensor_scalar(ymin[:, :, :], y[:, :, :], 0.0, None, ALU.min).then_inc(finish_step, 1)

            def put_result(pair, first=False):
                base = FINISH_STEPS * pair
                dve.wait_ge(xres_landed, 16 * pair + 16)
                dve.scalar_tensor_tensor(positive[:, :, :], y[:, :, :], 0.0, xres[:, :, :],
                                         ALU.max, ALU.add).then_inc(finish_step, 1)
                dve.wait_ge(finish_step, base + 9)
                dve.wait_ge(elu_exp, pair + 1)
                if not first:
                    dve.wait_ge(result_stored, 16 * pair)
                dve.scalar_tensor_tensor(result[:, :, :], yexp[:, :, :], -1.0, positive[:, :, :],
                                         ALU.add, ALU.add).then_inc(result_ready, 1)

            variances(0)
            inverse_roots(0)
            weights()
            variances(1)
            inverse_roots(1)
            weights_end()
            variances(2)
            bound()
            inverse_roots(2)
            variances(3)
            inverse_roots(3)
            s2_largest(0)
            s2_turn(0)
            s1_turn(0)
            evacuate((11,))
            s1_copy(0)
            edge_bytes(0, 0, first=True)
            evacuate((13,))
            s2_largest(1)
            s2_turn(1)
            evacuate((15,))
            edge_bytes(0, 1, first=True)
            s2_largest(2)
            s2_turn(2)
            s2_largest(3)
            dve.wait_ge(s2_maxima, XP)
            dve.reduce_max(small[:, 0:1], small[:, 8:12], AX.X).then_inc(s2_step, 1)
            s2_turn(3)
            dve.wait_ge(s2max_ready, 1)
            dve.tensor_scalar(small[:, 4:5], small[:, 1:2], -1.0, None, ALU.mult).then_inc(s2_step, 1)
            dve.tensor_scalar(small[:, 5:6], small[:, 1:2], -ALPHA, None, ALU.mult).then_inc(s2_step, 1)
            s1_turn(1)
            wait_evacuated(dve, G - 1)
            dve.reduce_sum(colmean[:, :], colsum[:, :], AX.X).then_inc(mean_step, 1)
            dve.wait_ge(mean_step, 1)
            dve.tensor_scalar(colmean_rep, ones[:, :], colmean[:, :], 1.0 / N,
                              ALU.mult, ALU.mult).then_inc(mean_step, 1)
            s1_copy(1)

            dve.wait_ge(bexp_ready, 2)
            dve.wait_ge(weights_step, 6)
            for w in range(2):
                dve.tensor_scalar(bscaled[:, w, :], bexp[:, w, :], small[:, 6:7], FP16_TOP,
                                  ALU.mult, ALU.mult).then_inc(bscaled_ready, 1)
            dve.wait_ge(bscaled_ready, 2)

            def scaled_factors(gr):
                dve.wait_ge(h_mm, gr + 1)
                if gr >= UVR:
                    dve.wait_ge(low_pool, lows_pool(gr - UVR))
                    dve.wait_ge(low_dve, lows_dve(gr - UVR))
                h4 = work[gr % 4][:, :].rearrange("p (k f) -> p k f", k=NK)
                for w in range(2):
                    factor = bscaled[:, w, NK * gr:NK * gr + NK].rearrange("p (k o) -> p k o", o=1)\
                        .to_broadcast([P, NK, F])
                    dve.tensor_tensor(uv32[gr % UVR][w], h4, factor, ALU.mult).then_inc(uv32_ready, 1)

            def low(gr):
                dve.wait_ge(high_ready, 2 * gr + 2)
                low_part(dve, gr, 1).then_inc(low_dve, 1)

            scaled_factors(0)
            s1_turn(2)
            codes(0, 0)
            denominators(0)
            low(0)
            scaled_factors(1)
            masks(0, 0, first=True)
            s1_copy(2)
            s1_turn(3)
            scaled_factors(2)
            scaled_factors(3)
            low(2)
            s1_copy(3)
            scaled_factors(4)
            codes(0, 1)
            low(4)
            scaled_factors(5)
            dve.wait_ge(mean_mm, 1)
            dve.tensor_copy(mean_h[:, :], mean_ps).then_inc(mean_step, 1)
            masks(0, 1, first=True)
            scaled_factors(6)
            edge_bytes(0, 2)
            scaled_factors(7)
            dve.wait_ge(h_mm, G // 2)
            denominators(1)
            scaled_factors(8)
            codes(0, 2)
            scaled_factors(9)
            masks(0, 2)
            edge_bytes(0, 3)
            scaled_factors(10)
            constants()
            scaled_factors(11)
            scaled_factors(12)
            codes(0, 3)
            scaled_factors(13)
            masks(0, 3)
            scaled_factors(14)
            scaled_factors(15)
            low(14)
            edge_bytes(1, 0)
            codes(1, 0)
            masks(1, 0)
            dve.wait_ge(aexp_ready, 2)
            dve.tensor_scalar(a_minus[:, :], a_minus[:, :], MINUS_RESCALE, None, ALU.mult).then_inc(aexp_ready, 1)
            dve.wait_ge(aexp_ready, 3)
            add_minus(0, 0)
            add_minus(1, 1)

            def iteration(n, first=False):
                if not first:
                    chunk(n, 0)
                chunk(n, 1)
                if not first:
                    add_minus(2 * n - 1, 1)
                finish(n - 1, first=first)
                chunk(n, 2)
                chunk(n, 3)
                put_result(n - 1, first=first)
                add_minus(2 * n, 0)

            iteration(1, first=True)
            with dve.Fori(2, NI) as n:
                iteration(n)
            add_minus(NB - 1, 1)
            finish(NI - 1)
            put_result(NI - 1)

        @block.tensor
        def _(pe):
            pe.wait_ge(w_landed, 48)
            pe.wait_ge(ident_ready, 2)
            pe.transpose(misc_ps[:, 0:F], w_sb[:, :], ident[:, :]).then_inc(pe_weights, 1)
            pe.wait_ge(weights_step, 2)
            pe.matmul(misc_ps[:, 256:256 + F], ones[:, :], w_sq, start=True, stop=True)\
                .then_inc(pe_weights, 1)
            pe.matmul(misc_ps[:, 128:130], w_t, a_sb[:, :], start=True, stop=True).then_inc(pe_weights, 1)

            def quarters_of(i):
                part = hn_t_low if i < 2 else hn_t_high[:, :, :]
                sets = part.rearrange("f m (k g b) -> f g (m k) b", k=NK, g=NQ)
                nodes = part.rearrange("f m (k g b) -> f g m b k", k=NK, g=NQ)
                first = GP * (i % 2)
                return sets[:, :, NK * first:NK * (first + GP), :], nodes[:, :, first:first + GP, :, :]

            def s2_along(i):
                wait_evacuated(pe, GP * i + GP - 1)
                if i >= 2:
                    pe.wait_ge(s2_copied, i - 1)
                for g in range(NQ):
                    ins = pe.matmul(s2_ps[i % 2][32 * g:32 * g + 32, :], wa_rep[:, 1, :],
                                    quarters_of(i)[0][:, g, :, :], start=True, stop=True)
                ins.then_inc(s2_mm, 1)

            def s1_along(i):
                if i:
                    pe.wait_ge(s1_transposed, i)
                for g in range(NQ):
                    ins = pe.matmul(s1_ps[32 * g:32 * g + 32, :], wa_rep[:, 0, :],
                                    quarters_of(i)[1][:, g, :, :, :], start=True, stop=True)
                ins.then_inc(s1_mm, 1)

            def s1_spread(i):
                pe.wait_ge(s1_transposed, i + 1)
                if i:
                    pe.wait_ge(s1bias_ready, i)
                pe.wait_ge(ident_ready, 2 + NQ * NQ)
                for g in range(NQ):
                    ins = pe.matmul(by_quarter(s1b_ps, i)[:, g, :], sel[:, g, :, :].rearrange("p q a -> p (q a)"),
                                    s1_turned[:, :, 0], start=True, stop=True)
                ins.then_inc(s1_spread_mm, 1)

            def h_group(gr):
                if gr >= 4:
                    pe.wait_ge(uv32_ready, 2 * gr - 6)
                for k in range(NK):
                    ins = pe.matmul(work[gr % 4][:, P * k:P * (k + 1)], hn_t[gr][:, P * k:P * (k + 1)],
                                    w_sb[:, :], start=True, stop=True)
                ins.then_inc(h_mm, 1)

            for gr in range(G):
                wait_normalised(pe, gr)
                if gr >= 4:
                    wait_evacuated(pe, gr - 4)
                for k in range(NQ):
                    ins = pe.transpose(work[gr % 4][:, P * k:P * (k + 1)], hn[:, gr % 4, k, :], ident[:, :])
                ins.then_inc(turned, 1)
                if gr == GP + 2:
                    pe.wait_ge(weights_step, 4)
                if gr == 9:
                    s1_along(0)
                if gr == 11:
                    s1_spread(0)
                if gr in (7, 11, 15):
                    s2_along(gr // GP - 1)
            s2_along(3)
            h_group(0)
            s1_along(1)
            h_group(1)
            h_group(2)
            s1_spread(1)
            s1_along(2)
            h_group(3)
            s1_spread(2)
            s1_along(3)

            plus8 = [plus[:, i, :].bitcast(dt.float8e4).rearrange("p (t i k) -> p t k i", t=NT, k=NK)
                     for i in range(2)]
            minus8 = [minus[:, i, :].bitcast(dt.float8e4).rearrange("p (t i k) -> p t k i", t=NT, k=NK)
                      for i in range(2)]

            def products(par, slot, gr):
                for k in range(NK):
                    j = NK * gr + k
                    ends = dict(start=(j == 0), stop=(j == NJ - 1))
                    pe.matmul(acc_plus[par][:, 0:2 * R], plus8[slot][:, gr % NT, k, :], uv[:, j, 0:2 * R], **ends)
                    ins = pe.matmul(acc_minus[par][:, 0:2 * R], minus8[slot][:, gr % NT, k, :],
                                    uv[:, j, 2 * R:4 * R], **ends)
                return ins

            def chunk(n, q):
                pe.wait_ge(masks_ready, 2 * CH * n + 2 * q + 2)
                pe.ldweights(uv[:, 0, 0:P], tile_position=(0, 0))
                for t in range(NT):
                    ins = products(q // NH, q % 2, NT * (q % NH) + t)
                ins.then_inc(chunk_summed, 1)

            pe.wait_ge(s2_copied, XP)
            BEHIND = 4

            def first_products(par, gr):
                pe.wait_ge(low_pool, lows_pool(gr))
                pe.wait_ge(low_dve, lows_dve(gr))
                if gr % NT == 0:
                    pe.wait_ge(den_ready, 4 * (gr // NT) + 4)
                    pe.wait_ge(masks_ready, 4 * (gr // NT) + 2 * par + 2)
                ins = products(par, par, gr)
                if gr % NT == NT - 1:
                    ins.then_inc(chunk_summed, 1)

            for first in range(0, G, NT):
                for gr in range(first, first + BEHIND):
                    if gr + 4 < G:
                        h_group(gr + 4)
                    first_products(0, gr)
                    if gr == 1:
                        s1_spread(3)
                if first == 0:
                    pe.wait_ge(mean_step, 2)
                    pe.wait_ge(s1bias_ready, XP)
                    pe.matmul(mean_ps, colmean_rep, w_sb[:, :], start=True, stop=True).then_inc(mean_mm, 1)
                    pe.wait_ge(mean_step, 3)
                for gr in range(first + BEHIND, first + NT):
                    if gr + 4 < G:
                        h_group(gr + 4)
                    first_products(0, gr)
                    first_products(1, gr - BEHIND)
                for gr in range(first + NT - BEHIND, first + NT):
                    first_products(1, gr)
            with pe.Fori(1, NI) as n:
                for q in range(CH):
                    if q % NH == 0:
                        pe.wait_ge(both_added, 2 * n + q // NH - 1)
                    chunk(n, q)


_INS = ['x', 'adj', 'L0_gnn_W', 'L0_gnn_a']


def kernel(**inputs):
    import numpy as _np
    import concourse.bacc as _bacc
    from concourse.bass_utils import run_bass_kernel_spmd as _run

    nc = _bacc.Bacc("TRN2", target_bir_lowering=False, num_devices=1)
    arrays, args = {}, []
    for name in _INS:
        arr = _np.ascontiguousarray(inputs[name])
        arrays[f"in_{name}_dram"] = arr
        args.append(nc.dram_tensor(f"in_{name}_dram", arr.shape, mybir.dt.from_np(arr.dtype),
                                   kind="ExternalInput").ap())
    args.append(nc.dram_tensor("out_dram", tuple(inputs['x'].shape), dt.float32, kind="ExternalOutput").ap())
    build(nc, *args)
    r = _run(nc, [arrays], core_ids=[0])
    return r.results[0]["out_dram"]
```
